# Optimizing a Trainium2 kernel written in Bass

```python
import numpy as np
import jax
import jax.numpy as jnp

def _softmax(x, axis=-1):
    return jax.nn.softmax(x, axis=axis)

def _gelu(x):
    return jax.nn.gelu(x, approximate=True)

def _silu(x):
    return jax.nn.silu(x)

def _sigmoid(x):
    return jax.nn.sigmoid(x)

def _layernorm(x, axis=-1, eps=1e-05):
    m = jnp.mean(x, axis=axis, keepdims=True)
    v = jnp.var(x, axis=axis, keepdims=True)
    return (x - m) / jnp.sqrt(v + eps)

def _scatter_add(tgt, idx, src, axis=0):
    return tgt.at[idx].add(src)

def _segment_sum(src, seg, n):
    return jax.ops.segment_sum(src, seg, n)
kernel_name = 'mk_vit_tower_d1_tok_img256_r4_304ad4'

def setup_inputs(seed: int=0):
    np.random.seed(seed)
    _w = jnp.asarray

    def _rec_inputs():
        import jax
        import jax.numpy as jnp
        _rk = jax.random.key(seed)
        x = 7.22013e-05 + 1.00017 * jax.random.normal(jax.random.fold_in(_rk, 1), (4, 64, 64, 64), jnp.float32)
        return x
    x = _rec_inputs()

    def _L0_tok_setup():
        import jax, jax.numpy as jnp
        import numpy as np
        K = 3
        PAD = (K - 1) // 2
        BN_EPS = 1e-05

        def _unfold(x):
            b, c, h, w = x.shape
            xp = jnp.pad(x, ((0, 0), (0, 0), (PAD, PAD), (PAD, PAD)))
            shifts = [xp[:, :, i:i + h, j:j + w] for i in range(K) for j in range(K)]
            return jnp.stack(shifts, axis=2)
        key = jax.random.key(seed)
        ks = jax.random.split(key, 4)
        b, c, h, w = (8, 64, 64, 64)
        cr = c // 4
        x = jax.random.normal(ks[0], (b, c, h, w), dtype=jnp.float32)
        conv1_w = jax.random.normal(ks[1], (cr, c), dtype=jnp.float32) * (1.0 / np.sqrt(c))
        conv1_b = jnp.zeros((cr,), dtype=jnp.float32)
        bn_gamma = jnp.ones((cr,), dtype=jnp.float32)
        bn_beta = jnp.zeros((cr,), dtype=jnp.float32)
        bn_mean = jnp.zeros((cr,), dtype=jnp.float32)
        bn_var = jnp.ones((cr,), dtype=jnp.float32)
        conv2_w = jax.random.normal(ks[2], (K * K, cr), dtype=jnp.float32) * (1.0 / np.sqrt(cr))
        conv2_b = jnp.zeros((K * K,), dtype=jnp.float32)
        return {'x': x, 'conv1_w': conv1_w, 'conv1_b': conv1_b, 'bn_gamma': bn_gamma, 'bn_beta': bn_beta, 'bn_mean': bn_mean, 'bn_var': bn_var, 'conv2_w': conv2_w, 'conv2_b': conv2_b}
    _L0_tok_all = _L0_tok_setup()
    _L0_tok_in = {k: v for k, v in _L0_tok_all.items() if k in ('conv1_w', 'conv1_b', 'bn_gamma', 'bn_beta', 'bn_mean', 'bn_var', 'conv2_w', 'conv2_b')}
    del _L0_tok_all

    def _L0_attn_setup():
        import jax, jax.numpy as jnp
        import numpy as np
        key = jax.random.key(seed)
        ks = jax.random.split(key, 4)
        B, S, D = (4, 1024, 64)
        x = jax.random.normal(ks[0], (B, S, D), dtype=jnp.float32)
        Wq = jax.random.normal(ks[1], (D, D), dtype=jnp.float32) * 0.02
        Wk = jax.random.normal(ks[2], (D, D), dtype=jnp.float32) * 0.02
        Wv = jax.random.normal(ks[3], (D, D), dtype=jnp.float32) * 0.02
        bq = jnp.zeros((D,), dtype=jnp.float32)
        bk = jnp.zeros((D,), dtype=jnp.float32)
        bv = jnp.zeros((D,), dtype=jnp.float32)
        return {'x': x, 'Wq': Wq, 'bq': bq, 'Wk': Wk, 'bk': bk, 'Wv': Wv, 'bv': bv}
    _L0_attn_all = _L0_attn_setup()
    _L0_attn_in = {k: v for k, v in _L0_attn_all.items() if k in ('Wq', 'bq', 'Wk', 'bk', 'Wv', 'bv')}
    del _L0_attn_all

    def _L0_ffn_setup():
        import jax, jax.numpy as jnp
        import numpy as np
        B, K, D = (128, 16, 64)
        E = 32
        H = int(D * 0.25)
        key = jax.random.key(seed)
        ks = jax.random.split(key, 7)
        d_rs = D ** (-0.5)
        h_rs = H ** (-0.5)
        x = jax.random.normal(ks[0], (B, K, D), dtype=jnp.float32)
        router_w = jax.random.uniform(ks[1], (E, D), jnp.float32, -d_rs, d_rs)
        router_b = jax.random.uniform(ks[2], (E,), jnp.float32, -d_rs, d_rs)
        W1 = jax.random.uniform(ks[3], (E, D, H), jnp.float32, -h_rs, h_rs)
        b1 = jax.random.uniform(ks[4], (E, H), jnp.float32, -h_rs, h_rs)
        W2 = jax.random.uniform(ks[5], (E, H, D), jnp.float32, -d_rs, d_rs)
        b2 = jax.random.uniform(ks[6], (E, D), jnp.float32, -d_rs, d_rs)
        return {'x': x, 'router_w': router_w, 'router_b': router_b, 'W1': W1, 'b1': b1, 'W2': W2, 'b2': b2}
    _L0_ffn_all = _L0_ffn_setup()
    _L0_ffn_in = {k: v for k, v in _L0_ffn_all.items() if k in ('router_w', 'router_b', 'W1', 'b1', 'W2', 'b2')}
    del _L0_ffn_all
    return {'x': x, 'L0_tok_conv1_w': _L0_tok_in['conv1_w'], 'L0_tok_conv1_b': _L0_tok_in['conv1_b'], 'L0_tok_bn_gamma': _L0_tok_in['bn_gamma'], 'L0_tok_bn_beta': _L0_tok_in['bn_beta'], 'L0_tok_bn_mean': _L0_tok_in['bn_mean'], 'L0_tok_bn_var': _L0_tok_in['bn_var'], 'L0_tok_conv2_w': _L0_tok_in['conv2_w'], 'L0_tok_conv2_b': _L0_tok_in['conv2_b'], 'L0_attn_Wq': _L0_attn_in['Wq'], 'L0_attn_bq': _L0_attn_in['bq'], 'L0_attn_Wk': _L0_attn_in['Wk'], 'L0_attn_bk': _L0_attn_in['bk'], 'L0_attn_Wv': _L0_attn_in['Wv'], 'L0_attn_bv': _L0_attn_in['bv'], 'L0_ffn_router_w': _L0_ffn_in['router_w'], 'L0_ffn_router_b': _L0_ffn_in['router_b'], 'L0_ffn_W1': _L0_ffn_in['W1'], 'L0_ffn_b1': _L0_ffn_in['b1'], 'L0_ffn_W2': _L0_ffn_in['W2'], 'L0_ffn_b2': _L0_ffn_in['b2']}

def reference(x, L0_tok_conv1_w, L0_tok_conv1_b, L0_tok_bn_gamma, L0_tok_bn_beta, L0_tok_bn_mean, L0_tok_bn_var, L0_tok_conv2_w, L0_tok_conv2_b, L0_attn_Wq, L0_attn_bq, L0_attn_Wk, L0_attn_bk, L0_attn_Wv, L0_attn_bv, L0_ffn_router_w, L0_ffn_router_b, L0_ffn_W1, L0_ffn_b1, L0_ffn_W2, L0_ffn_b2):
    import jax
    import jax.numpy as jnp

    def _L0_tok_ref(x, conv1_w, conv1_b, bn_gamma, bn_beta, bn_mean, bn_var, conv2_w, conv2_b):
        import jax, jax.numpy as jnp
        import numpy as np
        K = 3
        PAD = (K - 1) // 2
        BN_EPS = 1e-05

        def _unfold(x):
            b, c, h, w = x.shape
            xp = jnp.pad(x, ((0, 0), (0, 0), (PAD, PAD), (PAD, PAD)))
            shifts = [xp[:, :, i:i + h, j:j + w] for i in range(K) for j in range(K)]
            return jnp.stack(shifts, axis=2)
        b, c, h, w = x.shape
        y = jnp.einsum('oc,bchw->bohw', conv1_w, x) + conv1_b[None, :, None, None]
        y = (y - bn_mean[None, :, None, None]) * (bn_gamma[None, :, None, None] * jax.lax.rsqrt(bn_var + BN_EPS)[None, :, None, None]) + bn_beta[None, :, None, None]
        y = jax.nn.relu(y)
        wdyn = jnp.einsum('ok,bkhw->bohw', conv2_w, y) + conv2_b[None, :, None, None]
        patches = _unfold(x)
        out = jnp.einsum('bckhw,bkhw->bchw', patches, wdyn)
        return out.reshape(b, h * w, c)

    def _L0_attn_ref(x, Wq, bq, Wk, bk, Wv, bv):
        import jax, jax.numpy as jnp
        import numpy as np
        Q = jnp.einsum('bsd,de->bse', x, Wq) + bq
        K = jnp.einsum('bsd,de,->bse'.replace(',->', '->'), x, Wk) + bk
        V = jnp.einsum('bsd,de->bse', x, Wv) + bv
        scale = 1.0 / jnp.sqrt(jnp.asarray(Q.shape[-1], dtype=jnp.float32))
        scores = jnp.einsum('bqd,bkd->bqk', Q, K) * scale
        weights = jax.nn.softmax(scores, axis=-1)
        return jnp.einsum('bqk,bkd->bqd', weights, V)

    def _L0_ffn_ref(x, router_w, router_b, W1, b1, W2, b2):
        import jax, jax.numpy as jnp
        import numpy as np
        B, K, D = (128, 16, 64)
        E = 32
        H = int(D * 0.25)
        xf = x.reshape(-1, D)
        logits = xf @ router_w.T + router_b
        idx = jnp.argmax(logits, axis=-1)
        w1t = jnp.take(W1, idx, axis=0)
        h = jnp.einsum('nd,ndh->nh', xf, w1t) + jnp.take(b1, idx, axis=0)
        h = jax.nn.relu(h)
        w2t = jnp.take(W2, idx, axis=0)
        out = jnp.einsum('nh,nhd->nd', h, w2t) + jnp.take(b2, idx, axis=0)
        out = jax.nn.relu(out)
        return out.reshape(x.shape)
    h = _L0_tok_ref(x, L0_tok_conv1_w, L0_tok_conv1_b, L0_tok_bn_gamma, L0_tok_bn_beta, L0_tok_bn_mean, L0_tok_bn_var, L0_tok_conv2_w, L0_tok_conv2_b)
    h = h + _L0_attn_ref(_layernorm(h, axis=-1), L0_attn_Wq, L0_attn_bq, L0_attn_Wk, L0_attn_bk, L0_attn_Wv, L0_attn_bv)
    h = h + _L0_ffn_ref(_layernorm(h, axis=-1), L0_ffn_router_w, L0_ffn_router_b, L0_ffn_W1, L0_ffn_b1, L0_ffn_W2, L0_ffn_b2)
    return h

_drawn_inputs = setup_inputs


def setup_inputs(seed=0):
    import zlib

    import numpy as np

    out = dict(_drawn_inputs(seed))
    spreads = {'L0_tok_conv1_b': (0.0, 0.1),
     'L0_tok_bn_gamma': (1.0, 0.2),
     'L0_tok_bn_beta': (0.0, 0.1),
     'L0_tok_bn_mean': (0.0, 0.1),
     'L0_tok_bn_var': (1.0, 0.2),
     'L0_tok_conv2_b': (0.0, 0.1),
     'L0_attn_bq': (0.0, 0.8),
     'L0_attn_bk': (0.0, 0.8),
     'L0_attn_bv': (0.0, 0.1)}
    factors = {'L0_attn_Wq': 8.0, 'L0_attn_Wk': 8.0, 'L0_attn_Wv': 8.0, 'L0_ffn_b1': 6.271}
    for name, (base, spread) in spreads.items():
        noise = np.random.default_rng([zlib.crc32(name.encode()), seed]).standard_normal(out[name].shape)
        drawn = base * np.exp(spread * noise) if base else spread * noise
        out[name] = jnp.asarray(drawn.astype(out[name].dtype))
    for name, factor in factors.items():
        out[name] = (out[name] * factor).astype(out[name].dtype)
    return out
```

```python
import numpy as np
import concourse.bass as bass
from concourse import mybir
from contextlib import ExitStack
from typing import NamedTuple

F32 = mybir.dt.float32
F32R = mybir.dt.float32r
I32 = mybir.dt.int32
ALU = mybir.AluOpType
ACT = mybir.ActivationFunctionType
AX_X = mybir.AxisListType.X
ds = bass.ds

B, C, IMG, W = 4, 64, 64, 64
O, TAPS = 16, 9
D = W
HH = 2
TILES = IMG // HH
S = TILES * 128
QB = 1024
BT = QB // 128
NQ = S // QB
BLOCKS = B * NQ
E, H = 32, 16
FT = E * H // 128
RING = 4
SCALE = float(D) ** -0.5
EPS = 1e-5
BIG = 2.0 ** 100
RSQRT_SEED = float(0x5F3759DF)
SAFE_SCORE = 60.0
NORM_LIMIT = 2 * SAFE_SCORE ** 2 / (SCALE ** 2 * (D + 1))

ONCE = dict(w2c=TAPS * 128, wqm=128, wqb=128, wkm=128, wkb=128,
            w1m=E * H, w1b=E * H, mask=E * H, rm=E, rb=E, wvm=130, wvb=130)
KEPT = dict(ident=128, w1c=128, w2=FT * D, b2=D, desc=E, bn=5, b2c=TAPS, e0=128)


def columns(parts):
    at, out = 0, {}
    for name, n in parts.items():
        out[name] = (at, at + n)
        at += n
    return out, at


ONCE_AT, ONCE_N = columns(ONCE)
KEPT_AT, KEPT_N = columns(KEPT)

SLOTS = {
    1: ["c1", "pz0", "pz1"],
    2: ["tap0"],
    3: ["tap1", "tap2"],
    4: ["yt", "tap3"],
    5: ["tap4", "tap5"],
    6: ["lg", "tap6"],
    7: ["tap7", "tap8"],
    8: ["ot0", "ot1"],
    9: ["hid0", "hid1"],
    10: ["xt", "hid2"],
    11: ["hid3"],
    12: ["hid4", "hid5"],
    13: ["hid6", "hid7"],
    14: ["o2"],
    15: ["fin", "g0", "g1"],
    16: ["nm0", "nm1"],
}
PRE = ("c1", "tap", "xt", "g", "nm")
SPLIT = ("yt", "xt", "g")
NBANK = 3


def opening_slots():
    taps = [[f"tap{t}@{i}" for t in range(TAPS)] for i in range(NQ + 1)]

    def query_side(i):
        return [f"g0@{i}", f"g1@{i}"], [f"nm0@{i}", f"nm1@{i}"]

    g, nm = query_side(0)
    slots = {-1: ["c1@0", *taps[0], "c1@1", *taps[1][:2], "xt@0", taps[1][2], *g, taps[1][3], *nm]}
    for i in range(1, NQ + 1):
        g, nm = query_side(i - 1) if i > 1 else ([], [])
        s = (i - 1) * BT // 2
        slots[s + 0] = taps[i][2:6] if i > 1 else taps[i][4:6]
        slots[s + 1] = taps[i][6:8] + g
        slots[s + 2] = taps[i][8:] + ([f"c1@{i + 1}", *taps[i + 1][:2]] if i < NQ else [])
        slots[s + 3] = nm + ([f"xt@{i}"] if i < NQ else [])
    return slots


def base(name):
    return name.split("@")[0]


def other(name, stage):
    return stage + name[len(base(name)):]


class Body:

    def __init__(self, b, lo, hi, attend, post, pre, slots=SLOTS, before=None):
        self.b, self.lo, self.hi = b, lo, hi
        self.attend, self.post, self.pre = attend, post, pre
        self.slots = {g: [n for n in names if (pre if n.startswith(PRE) else post)]
                      for g, names in slots.items()}
        order = [n for g in sorted(self.slots) for n in self.slots[g]]
        self.bank, self.nth, self.high = {}, {}, {}
        self.per_bank, self.per_high = [0] * NBANK, 0
        for k, n in enumerate(order):
            self.bank[n] = k % NBANK
            self.nth[n] = self.per_bank[k % NBANK]
            self.per_bank[k % NBANK] += 1
            if n.startswith(SPLIT):
                self.high[n] = self.per_high
                self.per_high += 1 if n[0] == "g" else 2
        if before is None:
            self.start, self.start_high = [0] * NBANK, 0
        else:
            m = before.hi - before.lo
            self.start = [s + m * c for s, c in zip(before.start, before.per_bank)]
            self.start_high = before.start_high + m * before.per_high

    def fills_before(self, name, qb):
        k = self.bank[name]
        return (qb - self.lo) * self.per_bank[k] + (self.start[k] + self.nth[name])

    def highs_before(self, name, qb):
        return (qb - self.lo) * self.per_high + (self.start_high + self.high[name])

    def filled(self, name, qb):
        return self.fills_before(name, qb) + 1

    def highs(self, name, qb, part=0):
        return self.highs_before(name, qb) + (part + 1)

    def block(self, qb):
        return qb + NQ * self.b

    def posts(self, qb):
        return self.block(qb)

    def prepares(self, name, qb):
        if "@" in name:
            i = int(name.split("@")[1])
            return i // NQ, i % NQ, i + 1
        return self.b + 1, qb, self.block(qb) + (NQ + 1)


class Way(NamedTuple):
    scores_ready: object
    probs_ready: object
    pv_done: object


def later(count):
    return not isinstance(count, int) or count > 0


def bodies():
    end = {0: [f"{name}@{NQ}" for name in ("xt", "g0", "g1", "nm0", "nm1")]}
    spec = [(0, 0, 1, True, False, True, opening_slots()), (0, 0, 1, False, False, True, end)]
    for b in range(B):
        spec.append((b, 1 if b == 0 else 0, NQ, True, True, b < B - 1))
    spec.append((B, 0, 1, False, True, False))
    out = []
    for s in spec:
        out.append(Body(*s, before=out[-1] if out else None))
    return out


def vit_block_kernel(nc, x, once, kept, out):
    plan = bodies()
    opening, opening_end, *rest = plan
    epilogue = rest.pop()

    with ExitStack() as ctx:
        def sb(name, shape, dt=F32):
            return ctx.enter_context(nc.sbuf_tensor(name, shape, dt))

        def sem(name):
            return ctx.enter_context(nc.semaphore(name))

        xin = sb("xin", [128, 2, TILES + 2, W])
        hres = sb("hres", [128, 2 * TILES, D])
        tap_product = sb("tap_product", [128, 2, BT, W])
        conv1_split = sb("conv1_split", [128, 512], F32R)
        conv1_full = sb("conv1_full", [128, 512])
        xn_block = sb("xn_block", [128, BT, D])
        keys = sb("keys", [128, 2, TILES, D])
        last_keys = sb("last_keys", [128, 2, D])
        keys_t = sb("keys_t", [128, 2, S], F32R)
        g_high = sb("g_high", [128, S], F32R)
        g_low = sb("g_low", [128, S], F32R)
        probs = sb("probs", [128, RING, QB])
        z_sb = sb("z_sb", [128, 512])
        h2 = sb("h2", [128, BT, D])
        y_block = sb("y_block", [128, BT, D])
        y_t = sb("y_t", [128, QB], F32R)
        logits = sb("logits", [128, BT, E])
        pick = sb("pick", [128, BT, E])
        onehot = sb("onehot", [128, BT, E])
        onehot_t = sb("onehot_t", [128, QB], F32R)
        hidden = sb("hidden", [128, FT, QB])
        o2_sb = sb("o2_sb", [128, 512])
        out_sb = sb("out_sb", [128, BT, D])
        centred = sb("centred", [128, BT, D])
        squares = sb("squares", [128, BT, D])
        stat = sb("stat", [128, 8, BT])
        g_square = sb("g_square", [128, 2, 512], F32R)
        ones = sb("ones", [128, 128], F32R)
        norm_max = sb("norm_max", [128, 2, 2 * NQ])
        first_scale = sb("first_scale", [128, 1])
        flag = sb("flag", [128, 1], I32)
        g_tile = sb("g_tile", [128, 2, 128], F32R)
        max4 = sb("max4", [128, 2, 4])
        neg_max = sb("neg_max", [128, TILES])
        diag = sb("diag", [128, 2, 4, 128])
        w = sb("w", [128, KEPT_N])
        conv2_w = sb("conv2_w", [128, TAPS * 128], F32R)
        w1_high = sb("w1_high", [128, E * H], F32R)
        w1_low = sb("w1_low", [128, E * H], F32R)
        mask_w = sb("mask_w", [128, E * H], F32R)
        router_w = sb("router_w", [128, E, 2], F32R)
        wv_w = sb("wv_w", [128, 130])
        wqk = sb("wqk", [64, 2, 128])
        a_high = sb("a_high", [128, 128], F32R)
        a_low = sb("a_low", [128, 128], F32R)
        bn = sb("bn", [128, 8])

        w1_f = h2[:, :, :].rearrange("p t d -> p (t d)")
        router_f = pick[:, 0, :]
        staged = hidden[:, :, :].rearrange("p f n -> p (f n)")[:, 0:ONCE_N]
        load = {n: staged[:, a:z] for n, (a, z) in ONCE_AT.items()}
        keep = {n: w[:, a:z] for n, (a, z) in KEPT_AT.items()}
        ident = keep["ident"]
        w2 = keep["w2"].rearrange("p (f d) -> p f d", f=FT)

        scores = ctx.enter_context(nc.psum_tensor("scores", [128, 2, QB], F32))
        z_ps = ctx.enter_context(nc.psum_tensor("z_ps", [128, 512], F32))
        banks = [ctx.enter_context(nc.psum_tensor(f"bank{k}", [128, 512], F32)) for k in range(NBANK)]

        kept_loaded, once_loaded, once_rest_loaded = sem("kept_loaded"), sem("once_loaded"), sem("once_rest_loaded")
        x_first_loaded = sem("x_first_loaded")
        x_loaded = [sem("x_loaded0"), sem("x_loaded1")]
        qk_weights_ready, a_written, a_high_ready = sem("qk_weights_ready"), sem("a_written"), sem("a_high_ready")
        bn_ready, weights_ready = sem("bn_ready"), sem("weights_ready")
        constants_ready, pool_weights_ready = sem("constants_ready"), sem("pool_weights_ready")
        weights_high_ready = sem("weights_high_ready")
        filled = [sem(f"filled{k}") for k in range(NBANK)]
        drained = [sem(f"drained{k}") for k in range(NBANK)]
        high_ready = sem("high_ready")
        usual = Way(sem("scores_ready"), sem("probs_ready"), sem("pv_done"))
        again = Way(sem("scores_ready_again"), sem("probs_ready_again"), sem("pv_done_again"))
        z_copied = sem("z_copied")
        conv1_low_ready = sem("conv1_low_ready")
        xn_ready, keys_ready, last_keys_ready = sem("xn_ready"), sem("keys_ready"), sem("last_keys_ready")
        y_ready, onehot_ready = sem("y_ready"), sem("onehot_ready")
        out_ready, out_stored, out_sb_free = sem("out_ready"), sem("out_stored"), sem("out_sb_free")
        flag_ready, first_scale_ready = sem("flag_ready"), sem("first_scale_ready")
        g_tile_ready = sem("g_tile_ready")
        max_scores_ready, max_scores_read = sem("max_scores_ready"), sem("max_scores_read")
        diag_ready, shifted_ready = sem("diag_ready"), sem("shifted_ready")
        shifted_high_ready, shifted_split = sem("shifted_high_ready"), sem("shifted_split")

        block = ctx.enter_context(nc.Block())

        def by_parity(cols):
            return cols.rearrange("p (t a q) -> p t a q", a=2, q=128)

        def each_block(eng, body, run):
            if body.hi - body.lo == 1:
                run(body.lo)
            else:
                with eng.Fori(body.lo, body.hi) as qb:
                    run(qb)

        @block.sync
        def _(sp):
            def load_image(b, lo, hi, loaded):
                for half in range(HH):
                    r0, r1 = max(lo, 1 - half), min(hi, TILES + 2 - half)
                    i0 = half * TILES + r0 - 1
                    sp.dma_start(xin[half * C:(half + 1) * C, b % 2, r0:r1, :],
                                 x[b, :, i0:i0 + r1 - r0, :]).then_inc(loaded, 16)

            def store_block(body, qb):
                img = (qb + (NQ - 1)) // NQ + (body.b - 1)
                row = (qb + (NQ - 1)) % NQ
                sp.wait_ge(out_ready, body.posts(qb))
                for half in range(HH):
                    rows = out.rearrange("b (c h q t) w -> b q h c (t w)", c=C, h=HH, q=NQ)
                    sp.dma_start(rows[ds(img, 1), ds(row, 1), half, :, :].rearrange("b q c n -> (b q c) n"),
                                 out_sb[half * C:(half + 1) * C, :, :].rearrange("c t w -> c (t w)")
                                 ).then_inc(out_stored, 16)
                sp.wait_ge(out_stored, body.posts(qb) * 32)
                sp.sem_inc(out_sb_free, 1)

            sp.sem_inc(out_sb_free, 1)
            early = ONCE_AT["wkb"][1]
            sp.dma_start(w[:, :], kept).then_inc(kept_loaded, 16)
            load_image(0, 0, BT + 2, x_first_loaded)
            sp.dma_start(staged[:, 0:early], once[:, 0:early]).then_inc(once_loaded, 16)
            load_image(0, BT + 2, TILES + 2, x_loaded[0])
            sp.dma_start(staged[:, early:], once[:, early:]).then_inc(once_rest_loaded, 16)
            load_image(1, 0, TILES + 2, x_loaded[1])
            for body in rest:
                if 1 <= body.b and body.b + 1 < B:
                    sp.wait_ge(xn_ready, NQ * body.b)
                    load_image(body.b + 1, 0, TILES + 2, x_loaded[(body.b + 1) % 2])
                each_block(sp, body, lambda qb: store_block(body, qb))
            store_block(epilogue, 0)
            sp.wait_ge(out_stored, 32 * BLOCKS)

        @block.gpsimd
        def _(pool):
            P = nc.gpsimd
            P.memset(xn_block[:, :, 0:1], 1.0)
            P.memset(y_block[:, :, 0:1], 1.0)
            P.memset(ones[:, :].bitcast(F32), 1.0)
            pool.drain()
            P.engine_nop().then_inc(constants_ready, 1)
            P.memset(onehot_t[:, :].bitcast(F32), 0.0)
            pool.wait_ge(once_rest_loaded, 16)
            P.tensor_tensor(wv_w[:, :], load["wvm"], load["wvb"], ALU.subtract)
            P.tensor_tensor(router_f, load["rm"], load["rb"], ALU.subtract)
            P.tensor_tensor(w1_f, load["w1m"], load["w1b"], ALU.subtract)
            pool.drain()
            P.tensor_copy(router_w[:, :, 0], router_f)
            P.tensor_copy(w1_high[:, :], w1_f)
            P.tensor_copy(mask_w[:, :], load["mask"])
            pool.drain()
            P.tensor_tensor(router_w[:, :, 1], router_f, router_w[:, :, 0].bitcast(F32), ALU.subtract)
            P.tensor_tensor(w1_low[:, :], w1_f, w1_high[:, :].bitcast(F32), ALU.subtract)
            pool.drain()
            P.engine_nop().then_inc(pool_weights_ready, 1)

            def copy_keys(body, name, turn):
                img, qb, count = body.prepares(name, turn)
                pool.wait_ge(xn_ready, count)
                nc.gpsimd.tensor_copy(keys[:, img % 2, ds(qb * BT, BT), :],
                                      xn_block[:, :, :]).then_inc(keys_ready, 1)

            def copy_last_keys(b):
                if b:
                    pool.wait_ge(usual.pv_done, NQ * TILES * b)
                nc.gpsimd.tensor_copy(last_keys[:, :, :], keys[:, b % 2, TILES - 2:, :]).then_inc(last_keys_ready, 1)

            for i in range(NQ):
                copy_keys(opening, f"xt@{i}", 0)
            pool.wait_ge(keys_ready, NQ)
            copy_last_keys(0)
            copy_keys(opening, f"xt@{NQ}", 0)
            for body in rest:
                if body.b and body.b < B:
                    copy_last_keys(body.b)
                if body.pre:
                    each_block(pool, body, lambda qb: copy_keys(body, "xt", qb))

        @block.tensor
        def _(pe):
            def fill(body, full, turn):
                k = body.bank[full]
                bank = banks[k]
                name, qb = base(full), turn
                if name.startswith(PRE):
                    img, qb, prepared = body.prepares(full, turn)
                    par = img % 2
                before = body.fills_before(full, turn)
                if later(before):
                    pe.wait_ge(drained[k], before)
                if name == "c1":
                    if full == "c1@0":
                        pe.wait_ge(x_first_loaded, 32)
                    else:
                        pe.wait_ge(x_loaded[par], 32 * (img // 2 + 1))
                    last = nc.tensor.matmul(bank[:, :], keep["w1c"], xin[:, par, ds(qb * BT + 1, BT), :],
                                            start=True, stop=True)
                elif name.startswith("tap"):
                    t = int(name[3:])
                    if full == "tap0@0":
                        pe.wait_ge(weights_ready, 1)
                    if t == 0:
                        pe.wait_ge(conv1_low_ready, prepared)
                    last = nc.tensor.matmul(bank[:, :], conv2_w[:, t * 128:(t + 1) * 128], conv1_split[:, :],
                                            start=True, stop=True)
                elif name.startswith("pz"):
                    if name == "pz0":
                        pe.wait_ge(z_copied, body.posts(qb))
                    for j in range(2):
                        jj = 2 * int(name[2:]) + j
                        last = nc.tensor.matmul(bank[:, j * 130:(j + 1) * 130], z_sb[:, jj * 128:(jj + 1) * 128],
                                                wv_w[:, :], start=True, stop=True)
                elif name.startswith(("yt", "xt")):
                    src = y_block if name[0] == "y" else xn_block
                    if name == "yt":
                        pe.wait_ge(y_ready, body.posts(qb))
                    else:
                        pe.wait_ge(xn_ready, prepared)
                    for j in range(BT // 2):
                        last = nc.tensor.transpose(bank[:, j * 128:(j + 1) * 128],
                                                   src[:, 2 * j:2 * j + 2, :].rearrange("p a d -> p (a d)"), ident)
                elif name.startswith("g"):
                    c = int(name[1:])
                    xt = other(full, "xt")
                    pe.wait_ge(drained[body.bank[xt]], body.filled(xt, turn))
                    cols = keys_t[:, par, ds(qb * QB + c * 512, 512)]
                    nc.tensor.matmul(bank[:, :], a_high[:, :], cols, start=True, stop=False)
                    last = nc.tensor.matmul(bank[:, :], a_low[:, :], cols, start=False, stop=True)
                elif name.startswith("nm"):
                    c = int(name[2:])
                    pe.wait_ge(high_ready, body.highs(other(full, f"g{c}"), turn))
                    last = nc.tensor.matmul(bank[:, :], ones[:, :], g_square[:, c, :], start=True, stop=True)
                elif name == "lg":
                    pe.wait_ge(drained[body.bank["yt"]], body.filled("yt", qb))
                    for t in range(BT):
                        last = nc.tensor.matmul(bank[:, t * 64:(t + 1) * 64], y_t[:, t * 128:(t + 1) * 128],
                                                router_w[:, :, :].rearrange("p e s -> p (e s)"),
                                                start=True, stop=True)
                elif name.startswith("ot"):
                    if name == "ot0":
                        pe.wait_ge(onehot_ready, body.posts(qb))
                    for j in range(4):
                        last = nc.tensor.transpose(bank[0:E, j * 128:(j + 1) * 128],
                                                   onehot[:, 4 * int(name[2:]) + j, :], ident)
                elif name.startswith("hid"):
                    f, c = divmod(int(name[3:]), 2)
                    pe.wait_ge(drained[body.bank[f"ot{c}"]], body.filled(f"ot{c}", qb))
                    rows = slice(f * 128, (f + 1) * 128)
                    cols = slice(c * 512, (c + 1) * 512)
                    nc.tensor.matmul(bank[:, :], w1_high[:, rows], y_t[:, cols], start=True, stop=False)
                    nc.tensor.matmul(bank[:, :], w1_low[:, rows], y_t[:, cols], start=False, stop=False)
                    last = nc.tensor.matmul(bank[:, :], mask_w[:, rows], onehot_t[:, cols], start=False, stop=True)
                elif name == "o2":
                    for f in range(FT):
                        for c in range(2):
                            pe.wait_ge(drained[body.bank[f"hid{2 * f + c}"]], body.filled(f"hid{2 * f + c}", qb))
                            nc.tensor.matmul(bank[64 * c:64 * c + 64, :], w2[:, f, :],
                                             hidden[:, f, c * 512:(c + 1) * 512], start=(f == 0), stop=False)
                    for c in range(2):
                        last = nc.tensor.matmul(bank[64 * c:64 * c + 64, :], keep["b2"],
                                                onehot_t[:, c * 512:(c + 1) * 512].bitcast(F32),
                                                start=False, stop=True)
                else:
                    pe.wait_ge(drained[body.bank["o2"]], body.filled("o2", qb))
                    for j in range(4):
                        last = nc.tensor.transpose(bank[:, j * 128:(j + 1) * 128],
                                                   o2_sb[:, j * 128:(j + 1) * 128], ident)
                last.then_inc(filled[k], 1)

            def score(way, b, kt, qb, block):
                before = block * TILES + (kt - 1)
                if later(before):
                    pe.wait_ge(way.probs_ready, before)
                lhs = keys_t[:, b % 2, kt * 128:(kt + 1) * 128]
                for c in range(2):
                    cols = ds(qb * QB + c * 512, 512)
                    dst = scores[:, kt % 2, c * 512:(c + 1) * 512]
                    nc.tensor.matmul(dst, lhs, g_high[:, cols], start=True, stop=False)
                    last = nc.tensor.matmul(dst, lhs, g_low[:, cols], start=False, stop=True)
                last.then_inc(way.scores_ready, 1)

            def into_z(keys_of_tile, kt):
                for c in range(2):
                    last = nc.tensor.matmul(z_ps[64 * c:64 * c + 64, :], keys_of_tile,
                                            probs[:, kt % RING, c * 512:(c + 1) * 512],
                                            start=(kt == 0), stop=(kt == TILES - 1))
                return last

            def weigh(way, keys_of_tile, kt, block):
                if kt == 0 and later(block):
                    pe.wait_ge(z_copied, block)
                pe.wait_ge(way.probs_ready, block * TILES + (kt + 1))
                into_z(keys_of_tile, kt).then_inc(way.pv_done, 1)

            def run(body, qb):
                par = body.b % 2
                for name in body.slots.get(-1, []):
                    fill(body, name, qb)
                if body is opening:
                    for name in ("g0@0", "g1@0"):
                        pe.wait_ge(drained[body.bank[name]], body.filled(name, qb))
                for g in range(TILES // 2):
                    if body.attend:
                        if body is opening and g * 2 % BT == 0:
                            name = f"xt@{g * 2 // BT}"
                            pe.wait_ge(drained[body.bank[name]], body.filled(name, qb))
                        score(usual, body.b, 2 * g, qb, body.block(qb))
                        score(usual, body.b, 2 * g + 1, qb, body.block(qb))
                    if g == 0 and body.post:
                        pe.wait_ge(last_keys_ready, (body.block(qb) + (NQ - 1)) // NQ)
                        for u in range(2):
                            weigh(usual, last_keys[:, u, :], TILES - 2 + u, body.block(qb) - 1)
                    for name in body.slots.get(g, []):
                        fill(body, name, qb)
                    if body.attend and g:
                        if body is opening and (2 * g - 2) % BT == 0:
                            pe.wait_ge(keys_ready, (2 * g - 2) // BT + 1)
                        for kt in (2 * g - 2, 2 * g - 1):
                            weigh(usual, keys[:, par, kt, :], kt, body.block(qb))
                for name in body.slots.get(TILES // 2, []):
                    fill(body, name, qb)

            def attend_again():
                for kt in (TILES - 2, TILES - 1):
                    into_z(keys[:, 0, kt, :], kt)
                for kt in range(TILES):
                    score(again, 0, kt, 0, 0)
                    if 0 < kt < TILES - 1:
                        weigh(again, keys[:, 0, kt - 1, :], kt - 1, 0)
                pe.wait_ge(again.probs_ready, TILES)

            def find_max(b, after):
                def tile(r):
                    for u in range(2):
                        pe.wait_ge(g_tile_ready, (r + 16 * b) * 2 + (u + 1))
                        for part in range(4):
                            before = (r + 16 * b) * 8 + (4 * u + part - 1)
                            if later(before):
                                pe.wait_ge(max_scores_read, before)
                            for c in range(2):
                                k0 = part * QB + c * 512
                                last = nc.tensor.matmul(scores[:, part % 2, c * 512:(c + 1) * 512],
                                                        g_tile[:, u, :], keys_t[:, b % 2, k0:k0 + 512],
                                                        start=True, stop=True)
                            last.then_inc(max_scores_ready, 1)

                def shift(r):
                    for u in range(2):
                        pe.wait_ge(diag_ready, (r + 4 * b) * 2 + (u + 1))
                        before = (r + 4 * b) * 2 + (u - 1)
                        if later(before):
                            pe.wait_ge(shifted_split, before)
                        cols = keys_t[:, b % 2, ds(r * QB + u * 512, 512)]
                        nc.tensor.matmul(banks[u][:, :], a_high[:, :], cols, start=True, stop=False)
                        nc.tensor.matmul(banks[u][:, :], a_low[:, :], cols, start=False, stop=False)
                        nc.tensor.matmul(banks[u][:, :], keep["e0"],
                                         diag[:, u, :, :].rearrange("p j n -> p (j n)"),
                                         start=False, stop=True).then_inc(shifted_ready, 1)

                for k in range(NBANK):
                    pe.wait_ge(drained[k], after.start[k])
                pe.wait_ge(usual.probs_ready, max(TILES * NQ * b, TILES))
                tile(0)
                with pe.Fori(1, TILES // 2) as r:
                    tile(r)
                shift(0)
                with pe.Fori(1, NQ) as r:
                    shift(r)
                pe.wait_ge(max_scores_read, 128 * (b + 1))
                pe.wait_ge(shifted_split, 8 * (b + 1))

            def shift_if_needed(b, after):
                pe.wait_ge(flag_ready, b + 1)
                with pe.If(pe.value_load(flag[0:1, 0:1], min_val=0, max_val=1)):
                    find_max(b, after)
                    if b == 0:
                        attend_again()
                with pe.Else():
                    pe.sem_inc(max_scores_ready, 4 * TILES)
                    pe.sem_inc(shifted_ready, S // 512)

            pe.wait_ge(qk_weights_ready, 1)
            nc.tensor.matmul(z_ps[:, 0:128], wqk[:, 0, :], wqk[:, 1, :], start=True, stop=True).then_inc(a_written, 1)
            pe.wait_ge(kept_loaded, 16)

            run(opening, 0)
            shift_if_needed(0, opening_end)
            run(opening_end, 0)
            for body, before in zip(rest, [opening_end, *rest]):
                if 0 < body.b < B:
                    for name in ("xt", "g0", "g1"):
                        pe.wait_ge(drained[before.bank[name]], before.filled(name, NQ - 1))
                    pe.wait_ge(keys_ready, NQ * (body.b + 1))
                    shift_if_needed(body.b, body)
                each_block(pe, body, lambda qb: run(body, qb))
            run(epilogue, 0)

        @block.scalar
        def _(act):
            def drain(body, full, turn):
                k = body.bank[full]
                bank = banks[k]
                name, qb = base(full), turn
                if name.startswith(PRE):
                    img, qb, prepared = body.prepares(full, turn)
                    par = img % 2
                if name == "c1":
                    act.wait_ge(filled[k], body.filled(full, turn))
                    nc.scalar.activation(conv1_split[:, :], bank[:, :], ACT.Relu, bias=bn[:, 1:2], scale=bn[:, 0:1])
                    nc.scalar.activation(conv1_full[64:128, :], bank[64:128, :], ACT.Relu, bias=bn[64:128, 1:2],
                                         scale=bn[64:128, 0:1]).then_inc(drained[k], 1)
                elif name.startswith(("yt", "xt")):
                    act.wait_ge(filled[k], body.filled(full, turn))
                    dst = by_parity(y_t[0:64, :] if name[0] == "y" else keys_t[0:64, par, ds(qb * QB, QB)])
                    for odd in range(2):
                        nc.scalar.copy(dst[:, :, odd, :], bank[64 * odd:64 * odd + 64, :].rearrange(
                            "p (t q) -> p t q", q=128)).then_inc(high_ready, 1)
                elif name.startswith("g"):
                    act.wait_ge(filled[k], body.filled(full, turn))
                    c = int(name[1:])
                    nc.scalar.activation(g_square[:, c, :], bank[:, :], ACT.Square)
                    nc.scalar.copy(g_high[:, ds(qb * QB + c * 512, 512)], bank[:, :]).then_inc(high_ready, 1)
                elif name.startswith("ot"):
                    act.wait_ge(filled[k], body.filled(full, turn))
                    c = int(name[2:])
                    nc.scalar.copy(onehot_t[0:E, c * 512:(c + 1) * 512], bank[0:E, :]).then_inc(drained[k], 1)
                elif name.startswith("hid"):
                    act.wait_ge(filled[k], body.filled(full, turn))
                    f, c = divmod(int(name[3:]), 2)
                    nc.scalar.activation(hidden[:, f, c * 512:(c + 1) * 512], bank[:, :],
                                         ACT.Relu).then_inc(drained[k], 1)

            def exponentiate(way, kt, block, scale=SCALE):
                n = block * TILES
                act.wait_ge(way.scores_ready, n + (kt + 1))
                if later(n + (kt + 1 - RING)):
                    act.wait_ge(way.pv_done, n + (kt + 1 - RING))
                nc.scalar.activation(probs[:, kt % RING, :], scores[:, kt % 2, :], ACT.Exp,
                                     scale=scale).then_inc(way.probs_ready, 1)

            def run(body, qb):
                for g in range(-1, TILES // 2 + 1):
                    if body.attend and 0 <= g < TILES // 2:
                        for kt in (2 * g, 2 * g + 1):
                            if body is opening and kt == 0:
                                act.wait_ge(first_scale_ready, 1)
                            exponentiate(usual, kt, body.block(qb), first_scale[:, 0:1] if body is opening else SCALE)
                    for name in body.slots.get(g, []):
                        drain(body, name, qb)

            def find_max(b):
                def tile(r, first_tile):
                    for u in range(2):
                        if not first_tile:
                            act.wait_ge(max_scores_ready, (r + 16 * b) * 8 + (4 * u - 4))
                        nc.scalar.copy(g_tile[:, u, :], g_high[:, ds((r * 2 + u) * 128, 128)]
                                       ).then_inc(g_tile_ready, 1)

                def shift(r):
                    for u in range(2):
                        act.wait_ge(shifted_ready, (r + 4 * b) * 2 + (u + 1))
                        nc.scalar.copy(g_high[:, ds(r * QB + u * 512, 512)], banks[u][:, :]
                                       ).then_inc(shifted_high_ready, 1)

                act.drain()
                tile(0, True)
                with act.Fori(1, TILES // 2) as r:
                    tile(r, False)
                with act.Fori(0, NQ) as r:
                    shift(r)
                act.drain()

            def shift_if_needed(b):
                act.wait_ge(flag_ready, b + 1)
                with act.If(act.value_load(flag[0:1, 0:1], min_val=0, max_val=1)):
                    find_max(b)
                    if b == 0:
                        for kt in range(TILES):
                            exponentiate(again, kt, 0)
                with act.Else():
                    act.sem_inc(g_tile_ready, TILES)
                    act.sem_inc(shifted_high_ready, S // 512)

            act.wait_ge(once_loaded, 16)
            nc.scalar.copy(conv2_w[:, :], load["w2c"]).then_inc(weights_high_ready, 1)
            act.wait_ge(a_written, 1)
            nc.scalar.copy(a_high[:, :], z_ps[:, 0:128]).then_inc(a_high_ready, 1)
            act.wait_ge(bn_ready, 1)
            run(opening, 0)
            shift_if_needed(0)
            run(opening_end, 0)
            for body in rest:
                if 0 < body.b < B:
                    shift_if_needed(body.b)
                each_block(act, body, lambda qb: run(body, qb))
            run(epilogue, 0)

        @block.vector
        def _(dve):
            V = nc.vector

            def settle():
                dve.drain()

            def wide(v, n):
                return v.unsqueeze(v.ndim).broadcast_to([*v.shape, n])

            def rsqrt(dst, v, half):
                V.tensor_scalar(half.bitcast(I32), v.bitcast(I32), 1, None, ALU.logical_shift_right)
                settle()
                V.tensor_scalar(dst.bitcast(I32), half.bitcast(I32), -1.0, RSQRT_SEED, ALU.mult, ALU.add)
                settle()
                for _ in range(3):
                    V.scalar_tensor_tensor(half, dst, -0.5, dst, ALU.mult, ALU.mult)
                    settle()
                    V.tensor_tensor(half, half, v, ALU.mult)
                    settle()
                    V.scalar_tensor_tensor(dst, half, 1.5, dst, ALU.add, ALU.mult)
                    settle()

            total, var, scratch, rstd = (stat[:, k, :] for k in range(4))

            def normalise(src):
                V.reduce_sum(total, src, AX_X)
                settle()
                V.scalar_tensor_tensor(centred[:, :, :], wide(total, D), -1.0 / D, src, ALU.mult, ALU.add)
                settle()
                V.tensor_tensor(squares[:, :, :], centred[:, :, :], centred[:, :, :], ALU.mult)
                settle()
                V.reduce_sum(total, squares[:, :, :], AX_X)
                settle()
                V.tensor_scalar(var, total, 1.0 / D, EPS, ALU.mult, ALU.add)
                settle()
                rsqrt(rstd, var, scratch)

            def write_normalised(dst):
                return V.tensor_tensor(dst[:, :, 1:D], centred[:, :, 1:D], wide(rstd, D - 1), ALU.mult)

            def residual(body, qb):
                slot = qb + (NQ * (body.b % 2) + 2 * NQ - 1)
                return hres[:, ds(slot % (2 * NQ) * BT, BT), :]

            def layernorm(block, prepared):
                settle()
                normalise(block)
                if later(prepared - 1):
                    dve.wait_ge(keys_ready, prepared - 1)
                write_normalised(xn_block).then_inc(xn_ready, 1)

            def drain(body, full, turn):
                k = body.bank[full]
                bank = banks[k]
                name, qb = base(full), turn
                if name.startswith(PRE):
                    img, qb, prepared = body.prepares(full, turn)
                    par = img % 2
                if name == "c1":
                    dve.wait_ge(drained[k], body.filled(full, turn))
                    V.tensor_tensor(conv1_split[64:128, :], conv1_full[64:128, :],
                                    conv1_split[64:128, :].bitcast(F32), ALU.subtract).then_inc(conv1_low_ready, 1)
                    if body is opening and prepared > 1:
                        layernorm(hres[:, (prepared - 2) * BT:(prepared - 1) * BT, :], prepared - 1)
                elif name.startswith("tap"):
                    t = int(name[3:])
                    mine = hres[:, ds(qb * BT + par * TILES, BT), :]
                    dh, dw = divmod([4, 0, 1, 2, 3, 5, 6, 7, 8][t], 3)
                    lo, hi = max(0, 1 - dw), min(W, W + 1 - dw)
                    flt = bank[:, :].rearrange("p (r w) -> p r w", w=W)[:, :, lo:hi]
                    pix = xin[:, par, ds(qb * BT + dh, BT), lo + dw - 1:hi + dw - 1]
                    dst = mine if t == 0 else tap_product[:, t % 2, :, lo:hi]
                    if full == "tap0@0":
                        dve.wait_ge(x_first_loaded, 32)
                    elif t == 0:
                        dve.wait_ge(x_loaded[par], 32 * (img // 2 + 1))
                    dve.wait_ge(filled[k], body.filled(full, turn))
                    V.scalar_tensor_tensor(dst, flt, keep["b2c"][:, t:t + 1], pix, ALU.add,
                                           ALU.mult).then_inc(drained[k], 1)
                    settle()
                    if t:
                        V.tensor_tensor(mine[:, :, lo:hi], mine[:, :, lo:hi], dst, ALU.add)
                    if t == TAPS - 1 and (body is not opening or prepared == NQ + 1):
                        layernorm(mine, prepared)
                elif name.startswith(("yt", "xt")):
                    high, low = (by_parity(y_t[r, :] if name[0] == "y" else keys_t[r, par, ds(qb * QB, QB)])
                                 for r in (slice(0, 64), slice(64, 128)))
                    for odd in range(2):
                        dve.wait_ge(high_ready, body.highs(full, turn, odd))
                        last = V.tensor_tensor(low[:, :, odd, :], bank[64 * odd:64 * odd + 64, :].rearrange(
                            "p (t q) -> p t q", q=128), high[:, :, odd, :].bitcast(F32), ALU.subtract)
                    last.then_inc(drained[k], 1)
                elif name.startswith("g"):
                    cols = ds(qb * QB + int(name[1:]) * 512, 512)
                    dve.wait_ge(high_ready, body.highs(full, turn))
                    V.tensor_tensor(g_low[:, cols], bank[:, :], g_high[:, cols].bitcast(F32),
                                    ALU.subtract).then_inc(drained[k], 1)
                elif name.startswith("nm"):
                    dve.wait_ge(filled[k], body.filled(full, turn))
                    V.reduce_max(norm_max[:, par, ds(qb * 2 + int(name[2:]), 1)], bank[:, :],
                                 AX_X).then_inc(drained[k], 1)
                    if full == f"nm1@{NQ - 1}":
                        raise_flag(0)
                    elif full == "nm1@0":
                        worst = stat[:, 7, 0:1]
                        settle()
                        V.reduce_max(worst, norm_max[:, 0, 0:2], AX_X)
                        settle()
                        V.tensor_scalar(first_scale[:, :], worst, NORM_LIMIT, SCALE, ALU.is_le,
                                        ALU.mult).then_inc(first_scale_ready, 1)
                elif name.startswith("pz"):
                    n = int(name[2:])
                    dve.wait_ge(filled[k], body.filled(full, turn))
                    both = bank[:, 0:260].rearrange("p (j a w) -> p j a w", j=2, a=2)
                    rs = stat[:, 4, :].rearrange("p (a j) -> p j a", a=2)[:, 2 * n:2 * n + 2, :]
                    V.reciprocal(rs, both[:, :, :, D])
                    settle()
                    rows = h2[:, :, :].rearrange("p (a j) w -> p j a w", a=2)[:, 2 * n:2 * n + 2]
                    V.tensor_tensor(rows, both[:, :, :, 0:D], wide(rs, D), ALU.mult).then_inc(drained[k], 1)
                    if n:
                        settle()
                        V.tensor_tensor(h2[:, :, :], h2[:, :, :], residual(body, qb), ALU.add)
                        settle()
                        normalise(h2[:, :, :])
                        write_normalised(y_block).then_inc(y_ready, 1)
                elif name == "lg":
                    dve.wait_ge(filled[k], body.filled(full, turn))
                    V.reduce_sum(logits[:, :, :], bank[:, :].rearrange("p (t e s) -> p t e s", t=BT, s=2),
                                 AX_X).then_inc(drained[k], 1)
                    settle()
                    best = stat[:, 5, :]
                    V.reduce_max(best, logits[:, :, :], AX_X)
                    settle()
                    V.tensor_tensor(pick[:, :, :], logits[:, :, :], wide(best, E), ALU.is_ge)
                    settle()
                    V.tensor_tensor(pick[:, :, :], pick[:, :, :],
                                    keep["desc"].unsqueeze(1).broadcast_to([128, BT, E]), ALU.mult)
                    settle()
                    V.reduce_max(best, pick[:, :, :], AX_X)
                    settle()
                    V.tensor_tensor(onehot[:, :, :], pick[:, :, :], wide(best, E),
                                    ALU.is_equal).then_inc(onehot_ready, 1)
                elif name == "o2":
                    dve.wait_ge(filled[k], body.filled(full, turn))
                    V.tensor_copy(o2_sb[:, :], bank[:, :]).then_inc(drained[k], 1)
                elif name == "fin":
                    dve.wait_ge(filled[k], body.filled(full, turn))
                    dve.wait_ge(out_sb_free, body.posts(qb))
                    both = bank[:, :].rearrange("p (j a w) -> p j a w", j=4, a=2)
                    for a in range(2):
                        tiles = slice(4 * a, 4 * a + 4)
                        last = V.scalar_tensor_tensor(out_sb[:, tiles, :], both[:, :, a, :], 0.0, h2[:, tiles, :],
                                                      ALU.max, ALU.add)
                    last.then_inc(drained[k], 1)
                    settle()
                    V.engine_nop().then_inc(out_ready, 1)

            def run(body, qb):
                if body.post:
                    dve.wait_ge(usual.pv_done, body.posts(qb) * TILES)
                    V.tensor_copy(z_sb[:, :], z_ps[:, :]).then_inc(z_copied, 1)
                for g in range(-1, TILES // 2 + 1):
                    for name in body.slots.get(g, []):
                        drain(body, name, qb)

            def find_max(b):
                def tile(r):
                    for u in range(2):
                        for part in range(4):
                            dve.wait_ge(max_scores_ready, (r + 16 * b) * 8 + (4 * u + part + 1))
                            V.reduce_max(max4[:, u, part:part + 1], scores[:, part % 2, :],
                                         AX_X).then_inc(max_scores_read, 1)
                        settle()
                        V.tensor_reduce(neg_max[:, ds(r * 2 + u, 1)], max4[:, u, :], AX_X, ALU.max, negate=True)

                def shift(r):
                    for u in range(2):
                        if later((r + 4 * b) * 2 + (u - 1)):
                            dve.wait_ge(shifted_ready, (r + 4 * b) * 2 + (u - 1))
                        V.tensor_tensor(diag[:, u, :, :], ident.unsqueeze(1).broadcast_to([128, 4, 128]),
                                        wide(neg_max[:, ds((r * 2 + u) * 4, 4)], 128), ALU.mult
                                        ).then_inc(diag_ready, 1)
                    for u in range(2):
                        cols = ds(r * QB + u * 512, 512)
                        dve.wait_ge(shifted_high_ready, (r + 4 * b) * 2 + (u + 1))
                        V.tensor_tensor(g_low[:, cols], banks[u][:, :], g_high[:, cols].bitcast(F32),
                                        ALU.subtract).then_inc(shifted_split, 1)

                with dve.Fori(0, TILES // 2) as r:
                    tile(r)
                settle()
                shift(0)
                with dve.Fori(1, NQ) as r:
                    shift(r)

            def raise_flag(b):
                worst = stat[:, 6, 0:1]
                settle()
                V.reduce_max(worst, norm_max[:, b % 2, :], AX_X)
                settle()
                V.tensor_scalar(flag[:, :], worst, NORM_LIMIT, None, ALU.is_gt).then_inc(flag_ready, 1)

            def shift_if_needed(b):
                if b:
                    raise_flag(b)
                dve.wait_ge(flag_ready, b + 1)
                with dve.If(dve.value_load(flag[0:1, 0:1], min_val=0, max_val=1)):
                    find_max(b)
                with dve.Else():
                    dve.sem_inc(max_scores_read, 4 * TILES)
                    dve.sem_inc(diag_ready, S // 512)
                    dve.sem_inc(shifted_split, S // 512)

            for par in range(2):
                V.memset(xin[0:64, par, 0:1, :], 0.0)
                V.memset(xin[64:128, par, TILES + 1:TILES + 2, :], 0.0)
            dve.wait_ge(kept_loaded, 16)
            V.tensor_scalar(bn[:, 2:3], keep["bn"][:, 4:5], EPS, None, ALU.add)
            V.tensor_tensor(bn[:, 5:6], keep["bn"][:, 0:1], keep["bn"][:, 1:2], ALU.subtract)
            settle()
            rsqrt(bn[:, 3:4], bn[:, 2:3], bn[:, 4:5])
            V.tensor_tensor(bn[:, 0:1], bn[:, 3:4], keep["bn"][:, 2:3], ALU.mult)
            settle()
            V.scalar_tensor_tensor(bn[:, 1:2], bn[:, 5:6], bn[:, 0:1], keep["bn"][:, 3:4], ALU.mult,
                                   ALU.add).then_inc(bn_ready, 1)
            dve.wait_ge(once_loaded, 16)
            V.tensor_tensor(wqk[:, 0, :], load["wqm"][0:64], load["wqb"][0:64], ALU.subtract)
            V.tensor_tensor(wqk[:, 1, :], load["wkm"][0:64], load["wkb"][0:64],
                            ALU.subtract).then_inc(qk_weights_ready, 1)
            dve.wait_ge(weights_high_ready, 1)
            for p in (32, 96):
                rows = slice(p, p + 32)
                V.tensor_tensor(conv2_w[rows, :], load["w2c"][rows], conv2_w[rows, :].bitcast(F32), ALU.subtract)
            dve.wait_ge(a_high_ready, 1)
            V.tensor_tensor(a_low[:, :], z_ps[:, 0:128], a_high[:, :].bitcast(F32), ALU.subtract)
            settle()
            V.engine_nop().then_inc(weights_ready, 1)
            dve.wait_ge(constants_ready, 1)

            run(opening, 0)
            shift_if_needed(0)
            run(opening_end, 0)
            dve.wait_ge(pool_weights_ready, 1)
            for body in rest:
                if 0 < body.b < B:
                    shift_if_needed(body.b)
                each_block(dve, body, lambda qb: run(body, qb))
            run(epilogue, 0)


def _pack(parts, at, n):
    buf = np.zeros((128, n), np.float32)
    for name, a in parts.items():
        lo, hi = at[name]
        buf[:a.shape[0], lo:hi] = a.reshape(a.shape[0], -1)
    return buf


def _less_row0(w, bias):
    main, base = np.array(w), np.zeros_like(w)
    main[0] = bias
    base[1:] = w[0:1]
    return main, base


def kernel(**inputs):
    import concourse.bacc as _bacc
    from concourse.bass_utils import run_bass_kernel_spmd as _run

    a = {k: np.asarray(v) for k, v in inputs.items()}

    qm, qs = _less_row0(a["L0_attn_Wq"], a["L0_attn_bq"])
    km, ks = _less_row0(a["L0_attn_Wk"], a["L0_attn_bk"])
    vm, vs = _less_row0(a["L0_attn_Wv"], a["L0_attn_bv"])
    rm, rs = _less_row0(np.ascontiguousarray(a["L0_ffn_router_w"].T), a["L0_ffn_router_b"])
    w1 = np.ascontiguousarray(a["L0_ffn_W1"].transpose(1, 0, 2)).reshape(D, E * H)
    w1m, w1s = _less_row0(w1, a["L0_ffn_b1"].reshape(-1))

    def twice(m, axis):
        return np.concatenate([m, m], axis)

    def value_diag(m, one):
        v = np.zeros((128, 130), np.float32)
        for k in range(2):
            v[64 * k:64 * k + 64, 65 * k:65 * k + 64] = m
            v[64 * k, 65 * k + 64] = one
        return v

    order = [4, 0, 1, 2, 3, 5, 6, 7, 8]
    w2c = np.zeros((4, HH, O, TAPS, HH, C), np.float32)
    w1c = np.zeros((HH, C, 4, HH, O), np.float32)
    for h in range(HH):
        w2c[:, h, :, :, h, :] = a["L0_tok_conv2_w"][order].T[None, :, :, None]
        w1c[h, :, :, h, :] = a["L0_tok_conv1_w"].T[:, None, :]
    mask = np.full((E, E, H), -BIG, np.float32)
    mask[np.arange(E), np.arange(E)] = 0.0
    bn = np.stack([a["L0_tok_" + n] for n in ("conv1_b", "bn_mean", "bn_gamma", "bn_beta", "bn_var")], 1)
    e0 = np.zeros((128, 128), np.float32)
    e0[:, 0] = e0[:, 64] = 1.0

    once = _pack(dict(w2c=w2c.reshape(128, -1), w1m=twice(w1m, 0), w1b=twice(w1s, 0),
                      mask=mask.reshape(E, E * H), rm=twice(rm, 0), rb=twice(rs, 0),
                      wvm=value_diag(vm, 1.0), wvb=value_diag(vs, 0.0),
                      wqm=twice(qm.T, 1), wqb=twice(qs.T, 1), wkm=twice(km.T, 1), wkb=twice(ks.T, 1)),
                 ONCE_AT, ONCE_N)
    w2 = a["L0_ffn_W2"].reshape(FT, 128, D).transpose(1, 0, 2)
    kept = _pack(dict(ident=np.eye(128, dtype=np.float32), w1c=w1c.reshape(128, 128), w2=w2,
                      b2=a["L0_ffn_b2"], desc=np.tile(np.arange(E, 0, -1, dtype=np.float32), (128, 1)),
                      bn=np.tile(bn, (8, 1)), b2c=np.tile(a["L0_tok_conv2_b"][order], (128, 1)), e0=e0),
                 KEPT_AT, KEPT_N)

    nc = _bacc.Bacc("TRN2", target_bir_lowering=False, num_devices=1)
    arrays = {"x_dram": np.ascontiguousarray(a["x"]), "once_dram": once, "kept_dram": kept}
    args = [nc.dram_tensor(n, v.shape, F32, kind="ExternalInput").ap() for n, v in arrays.items()]
    out = nc.dram_tensor("out_dram", (B, S, D), F32, kind="ExternalOutput").ap()
    vit_block_kernel(nc, *args, out)
    r = _run(nc, [arrays], core_ids=[0])
    return r.results[0]["out_dram"]
```

```python
import numpy as np
import concourse.bass as bass
from concourse import mybir
from contextlib import ExitStack
from typing import NamedTuple

F32 = mybir.dt.float32
F32R = mybir.dt.float32r
I32 = mybir.dt.int32
ALU = mybir.AluOpType
ACT = mybir.ActivationFunctionType
AX_X = mybir.AxisListType.X
ds = bass.ds

B, C, IMG, W = 4, 64, 64, 64
O, TAPS = 16, 9
D = W
HH = 2
TILES = IMG // HH
S = TILES * 128
QB = 1024
BT = QB // 128
NQ = S // QB
BLOCKS = B * NQ
E, H = 32, 16
FT = E * H // 128
RING = 4
SCALE = float(D) ** -0.5
EPS = 1e-5
BIG = 2.0 ** 100
RSQRT_SEED = float(0x5F3759DF)
SAFE_SCORE = 60.0
NORM_LIMIT = 2 * SAFE_SCORE ** 2 / (SCALE ** 2 * (D + 1))

ONCE = dict(w2c=TAPS * 128, wqm=128, wqb=128, wkm=128, wkb=128,
            w1m=E * H, w1b=E * H, mask=E * H, rm=E, rb=E, wvm=130, wvb=130)
KEPT = dict(w1c=128, bn=5, b2c=TAPS, ident=128, w2=FT * D, b2=D, desc=E, e0=128)


def columns(parts):
    at, out = 0, {}
    for name, n in parts.items():
        out[name] = (at, at + n)
        at += n
    return out, at


ONCE_AT, ONCE_N = columns(ONCE)
KEPT_AT, KEPT_N = columns(KEPT)

SLOTS = {
    1: ["c1", "pz0", "pz1"],
    2: ["tap0"],
    3: ["tap1", "tap2"],
    4: ["yt"],
    5: ["tap3", "tap4", "tap5"],
    6: ["tap6", "lg"],
    7: ["tap7", "tap8"],
    8: ["ot"],
    9: ["hid0", "hid1"],
    10: ["hid2", "xt"],
    11: ["hid3", "g0", "g1"],
    12: ["hid4", "hid5"],
    13: ["nm0", "nm1", "hid6"],
    14: ["hid7", "o2"],
    16: ["fin"],
}
PRE = ("c1", "tap", "xt", "g", "nm")
SPLIT = ("yt", "xt", "g")
NBANK = 3


def fills(*parts):
    return [f"{name}@{i}" for i, names in parts for name in names.split()]


def opening_slots():
    taps = " ".join(f"tap{t}" for t in range(TAPS))
    return {
        -1: fills((0, "c1 " + taps), (1, "c1 tap0 tap1"), (0, "xt"), (1, "tap2"), (0, "g0 g1"), (1, "tap3"),
                  (0, "nm0 nm1")),
        0: fills((1, "tap4 tap5")),
        1: fills((1, "tap6")),
        2: fills((1, "tap7 tap8"), (2, "c1 tap0 tap1")),
        3: fills((1, "xt")),
        4: fills((2, "tap2 tap3 tap4 tap5")),
        5: fills((2, "tap6 tap7"), (1, "g0 g1")),
        6: fills((2, "tap8"), (3, "c1 tap0 tap1"), (1, "nm0")),
        7: fills((1, "nm1"), (2, "xt")),
        8: fills((3, "tap2 tap3 tap4")),
        9: fills((3, "tap5 tap6 tap7"), (2, "g0 g1"), (3, "tap8")),
        11: fills((2, "nm0 nm1"), (3, "xt")),
        12: fills((3, "g0")),
        13: fills((3, "g1 nm0 nm1")),
    }


def second_slots():
    return {
        1: [*fills((4, "c1")), "pz0", "pz1"],
        2: fills((4, "tap0")),
        3: fills((4, "tap1 tap2")),
        4: [*fills((4, "tap3")), "yt", *fills((4, "tap4 tap5"))],
        5: fills((4, "tap6 tap7")),
        6: ["lg", *fills((4, "tap8"))],
        7: ["c1"],
        8: ["tap0", "ot", "tap1"],
        9: [*fills((4, "xt")), "hid0", "tap2"],
        10: ["tap3", "hid1"],
        11: [*fills((4, "g0 g1")), "hid2", "tap4"],
        12: [*fills((4, "nm0 nm1")), "hid3", "tap5"],
        13: ["hid4", "tap6", "hid5", "tap7"],
        14: ["hid6", "hid7", "tap8"],
        15: ["o2"],
        16: ["fin", "xt", "g0", "g1", "nm0", "nm1"],
    }


def base(name):
    return name.split("@")[0]


def other(name, stage):
    return stage + name[len(base(name)):]


class Body:

    def __init__(self, b, lo, hi, attend, post, pre, slots=SLOTS, before=None):
        self.b, self.lo, self.hi = b, lo, hi
        self.attend, self.post, self.pre = attend, post, pre
        self.slots = {g: [n for n in names if (pre if n.startswith(PRE) else post)]
                      for g, names in slots.items()}
        order = [n for g in sorted(self.slots) for n in self.slots[g]]
        self.bank, self.nth, self.high = {}, {}, {}
        self.per_bank, self.per_high = [0] * NBANK, 0
        for k, n in enumerate(order):
            self.bank[n] = k % NBANK
            self.nth[n] = self.per_bank[k % NBANK]
            self.per_bank[k % NBANK] += 1
            if n.startswith(SPLIT):
                self.high[n] = self.per_high
                self.per_high += 1 if n[0] == "g" else 2
        if before is None:
            self.start, self.start_high = [0] * NBANK, 0
        else:
            m = before.hi - before.lo
            self.start = [s + m * c for s, c in zip(before.start, before.per_bank)]
            self.start_high = before.start_high + m * before.per_high

    def fills_before(self, name, qb):
        k = self.bank[name]
        return (qb - self.lo) * self.per_bank[k] + (self.start[k] + self.nth[name])

    def highs_before(self, name, qb):
        return (qb - self.lo) * self.per_high + (self.start_high + self.high[name])

    def filled(self, name, qb):
        return self.fills_before(name, qb) + 1

    def highs(self, name, qb, part=0):
        return self.highs_before(name, qb) + (part + 1)

    def block(self, qb):
        return qb + NQ * self.b

    def posts(self, qb):
        return self.block(qb)

    def prepares(self, name, qb):
        if "@" in name:
            i = int(name.split("@")[1])
            return i // NQ, i % NQ, i + 1
        return self.b + 1, qb, self.block(qb) + (NQ + 1)


class Way(NamedTuple):
    scores_ready: object
    probs_ready: object
    pv_done: object


def later(count):
    return not isinstance(count, int) or count > 0


def bodies():
    spec = [(0, 0, 1, True, False, True, opening_slots()), (0, 1, 2, True, True, True, second_slots())]
    for b in range(B):
        spec.append((b, 2 if b == 0 else 0, NQ, True, True, b < B - 1))
    spec.append((B, 0, 1, False, True, False))
    out = []
    for s in spec:
        out.append(Body(*s, before=out[-1] if out else None))
    return out


def vit_block_kernel(nc, x, once, kept, out):
    plan = bodies()
    opening, *rest = plan
    epilogue = rest.pop()

    with ExitStack() as ctx:
        def sb(name, shape, dt=F32):
            return ctx.enter_context(nc.sbuf_tensor(name, shape, dt))

        def sem(name):
            return ctx.enter_context(nc.semaphore(name))

        xin = sb("xin", [128, 2, TILES + 2, W])
        hres = sb("hres", [128, 2 * TILES, D])
        tap_product = sb("tap_product", [128, 2, BT, W])
        conv1_split = sb("conv1_split", [128, 512], F32R)
        conv1_full = sb("conv1_full", [128, 512])
        xn_block = sb("xn_block", [128, BT, D])
        keys = sb("keys", [128, 2, TILES, D])
        last_keys = sb("last_keys", [128, 2, D])
        keys_t = sb("keys_t", [128, 2, S], F32R)
        g_high = sb("g_high", [128, (NQ + 1) * QB], F32R)
        g_low = sb("g_low", [128, (NQ + 1) * QB], F32R)
        probs = sb("probs", [128, RING, QB])
        z_sb = sb("z_sb", [128, 512])
        h2 = sb("h2", [128, BT, D])
        y_block = sb("y_block", [128, BT, D])
        y_t = sb("y_t", [128, QB], F32R)
        logits = sb("logits", [128, BT, E])
        pick = sb("pick", [128, BT, E])
        onehot = sb("onehot", [128, BT, E])
        onehot_t = sb("onehot_t", [128, QB], F32R)
        hidden = sb("hidden", [128, FT, QB])
        o2_sb = sb("o2_sb", [128, 512])
        out_sb = sb("out_sb", [128, BT, D])
        stat = sb("stat", [128, 8, BT])
        g_square = sb("g_square", [128, 2, 512], F32R)
        ones = sb("ones", [128, 128], F32R)
        norm_max = sb("norm_max", [128, 2, 2 * NQ])
        first_scale = sb("first_scale", [128, 1])
        flag = sb("flag", [128, 1], I32)
        g_tile = sb("g_tile", [128, 2, 128], F32R)
        max4 = sb("max4", [128, 2, 4])
        neg_max = sb("neg_max", [128, TILES])
        w = sb("w", [128, KEPT_N])
        conv2_w = sb("conv2_w", [128, TAPS * 128], F32R)
        w1_high = sb("w1_high", [128, E * H], F32R)
        w1_low = sb("w1_low", [128, E * H], F32R)
        mask_w = sb("mask_w", [128, E * H], F32R)
        router_w = sb("router_w", [128, E, 2], F32R)
        wv_w = sb("wv_w", [128, 130])
        wqk = sb("wqk", [64, 2, 128])
        a_high = sb("a_high", [128, 128], F32R)
        a_low = sb("a_low", [128, 128], F32R)
        bn = sb("bn", [128, 8])

        centred, squares = tap_product[:, 0], tap_product[:, 1]
        diag = hidden[:, 0, :].rearrange("p (u j n) -> p u j n", u=2, j=4)
        w1_f = h2[:, :, :].rearrange("p t d -> p (t d)")
        router_f = pick[:, 0, :]
        staged = hidden[:, :, :].rearrange("p f n -> p (f n)")[:, 0:ONCE_N]
        load = {n: staged[:, a:z] for n, (a, z) in ONCE_AT.items()}
        keep = {n: w[:, a:z] for n, (a, z) in KEPT_AT.items()}
        ident = keep["ident"]
        w2 = keep["w2"].rearrange("p (f d) -> p f d", f=FT)

        scores = ctx.enter_context(nc.psum_tensor("scores", [128, 2, QB], F32))
        z_ps = ctx.enter_context(nc.psum_tensor("z_ps", [128, 512], F32))
        banks = [ctx.enter_context(nc.psum_tensor(f"bank{k}", [128, 512], F32)) for k in range(NBANK)]

        kept_loaded, once_loaded, once_rest_loaded = sem("kept_loaded"), sem("once_loaded"), sem("once_rest_loaded")
        kept_first_loaded, qk_loaded = sem("kept_first_loaded"), sem("qk_loaded")
        x_first_loaded = sem("x_first_loaded")
        x_loaded = [sem("x_loaded0"), sem("x_loaded1")]
        qk_weights_ready, a_written, a_high_ready = sem("qk_weights_ready"), sem("a_written"), sem("a_high_ready")
        bn_ready, conv2_ready, a_ready = sem("bn_ready"), sem("conv2_ready"), sem("a_ready")
        constants_ready, pool_weights_ready = sem("constants_ready"), sem("pool_weights_ready")
        weights_high_ready = sem("weights_high_ready")
        filled = [sem(f"filled{k}") for k in range(NBANK)]
        drained = [sem(f"drained{k}") for k in range(NBANK)]
        high_ready = sem("high_ready")
        usual = Way(sem("scores_ready"), sem("probs_ready"), sem("pv_done"))
        again = Way(sem("scores_ready_again"), sem("probs_ready_again"), sem("pv_done_again"))
        z_copied = sem("z_copied")
        conv1_low_ready = sem("conv1_low_ready")
        xn_ready, keys_ready, last_keys_ready = sem("xn_ready"), sem("keys_ready"), sem("last_keys_ready")
        y_ready, onehot_ready = sem("y_ready"), sem("onehot_ready")
        out_ready, out_stored, out_sb_free = sem("out_ready"), sem("out_stored"), sem("out_sb_free")
        flag_ready, first_scale_ready = sem("flag_ready"), sem("first_scale_ready")
        g_tile_ready = sem("g_tile_ready")
        max_scores_ready, max_scores_read = sem("max_scores_ready"), sem("max_scores_read")
        diag_ready, shifted_ready = sem("diag_ready"), sem("shifted_ready")
        shifted_high_ready, shifted_split = sem("shifted_high_ready"), sem("shifted_split")

        block = ctx.enter_context(nc.Block())

        def by_parity(cols):
            return cols.rearrange("p (t a q) -> p t a q", a=2, q=128)

        def query_cols(block, chunk):
            return ds(block % (NQ + 1) * QB + chunk * 512, 512)

        def each_block(eng, body, run):
            if body.hi - body.lo == 1:
                run(body.lo)
            else:
                with eng.Fori(body.lo, body.hi) as qb:
                    run(qb)

        @block.sync
        def _(sp):
            def load_image(b, lo, hi, loaded):
                for half in range(HH):
                    r0, r1 = max(lo, 1 - half), min(hi, TILES + 2 - half)
                    i0 = half * TILES + r0 - 1
                    sp.dma_start(xin[half * C:(half + 1) * C, b % 2, r0:r1, :],
                                 x[b, :, i0:i0 + r1 - r0, :]).then_inc(loaded, 16)

            def store_block(body, qb):
                img = (qb + (NQ - 1)) // NQ + (body.b - 1)
                row = (qb + (NQ - 1)) % NQ
                sp.wait_ge(out_ready, body.posts(qb))
                for half in range(HH):
                    rows = out.rearrange("b (c h q t) w -> b q h c (t w)", c=C, h=HH, q=NQ)
                    sp.dma_start(rows[ds(img, 1), ds(row, 1), half, :, :].rearrange("b q c n -> (b q c) n"),
                                 out_sb[half * C:(half + 1) * C, :, :].rearrange("c t w -> c (t w)")
                                 ).then_inc(out_stored, 16)
                sp.wait_ge(out_stored, body.posts(qb) * 32)
                sp.sem_inc(out_sb_free, 1)

            sp.sem_inc(out_sb_free, 1)
            first, taps, rest_of_it = KEPT_AT["b2c"][1], ONCE_AT["w2c"][1], ONCE_AT["wkb"][1]
            sp.dma_start(w[:, 0:first], kept[:, 0:first]).then_inc(kept_first_loaded, 16)
            sp.dma_start(staged[:, 0:taps], once[:, 0:taps]).then_inc(once_loaded, 16)
            load_image(0, 0, BT + 2, x_first_loaded)
            sp.dma_start(staged[0:D, taps:rest_of_it], once[0:D, taps:rest_of_it]).then_inc(qk_loaded, 16)
            sp.dma_start(w[:, first:], kept[:, first:]).then_inc(kept_loaded, 16)
            load_image(0, BT + 2, TILES + 2, x_loaded[0])
            sp.dma_start(staged[:, rest_of_it:], once[:, rest_of_it:]).then_inc(once_rest_loaded, 16)
            load_image(1, 0, TILES + 2, x_loaded[1])
            for body in rest:
                if body is rest[0] or body.lo == 0 and 1 <= body.b < B - 2:
                    sp.wait_ge(xn_ready, NQ * (body.b + 1))
                    load_image(body.b + 2, 0, TILES + 2, x_loaded[body.b % 2])
                each_block(sp, body, lambda qb: store_block(body, qb))
            store_block(epilogue, 0)
            sp.wait_ge(out_stored, 32 * BLOCKS)

        @block.gpsimd
        def _(pool):
            P = nc.gpsimd
            P.memset(xn_block[:, :, 0:1], 1.0)
            P.memset(y_block[:, :, 0:1], 1.0)
            P.memset(ones[:, :].bitcast(F32), 1.0)
            P.memset(norm_max[:, :, :], 0.0)
            pool.drain()
            P.engine_nop().then_inc(constants_ready, 1)
            P.memset(onehot_t[:, :].bitcast(F32), 0.0)
            pool.wait_ge(once_rest_loaded, 16)
            P.tensor_tensor(wv_w[:, :], load["wvm"], load["wvb"], ALU.subtract)
            P.tensor_tensor(router_f, load["rm"], load["rb"], ALU.subtract)
            P.tensor_tensor(w1_f, load["w1m"], load["w1b"], ALU.subtract)
            pool.drain()
            P.tensor_copy(router_w[:, :, 0], router_f)
            P.tensor_copy(w1_high[:, :], w1_f)
            P.tensor_copy(mask_w[:, :], load["mask"])
            pool.drain()
            P.tensor_tensor(router_w[:, :, 1], router_f, router_w[:, :, 0].bitcast(F32), ALU.subtract)
            P.tensor_tensor(w1_low[:, :], w1_f, w1_high[:, :].bitcast(F32), ALU.subtract)
            pool.drain()
            P.engine_nop().then_inc(pool_weights_ready, 1)

            def copy_keys(body, name, turn):
                img, qb, count = body.prepares(name, turn)
                pool.wait_ge(xn_ready, count)
                nc.gpsimd.tensor_copy(keys[:, img % 2, ds(qb * BT, BT), :],
                                      xn_block[:, :, :]).then_inc(keys_ready, 1)

            def copy_last_keys(b):
                if b:
                    pool.wait_ge(usual.pv_done, NQ * TILES * b)
                nc.gpsimd.tensor_copy(last_keys[:, :, :], keys[:, b % 2, TILES - 2:, :]).then_inc(last_keys_ready, 1)

            for i in range(NQ):
                copy_keys(opening, f"xt@{i}", 0)
            pool.wait_ge(keys_ready, NQ)
            copy_last_keys(0)
            copy_keys(rest[0], f"xt@{NQ}", 1)
            for body in rest:
                if body.b and body.b < B:
                    copy_last_keys(body.b)
                if body.pre:
                    each_block(pool, body, lambda qb: copy_keys(body, "xt", qb))

        @block.tensor
        def _(pe):
            def fill(body, full, turn):
                k = body.bank[full]
                bank = banks[k]
                name, qb = base(full), turn
                if name.startswith(PRE):
                    img, qb, prepared = body.prepares(full, turn)
                    par = img % 2
                before = body.fills_before(full, turn)
                if later(before):
                    pe.wait_ge(drained[k], before)
                if name == "c1":
                    if full == "c1@0":
                        pe.wait_ge(x_first_loaded, 32)
                    elif full == "c1@1":
                        pe.wait_ge(qk_weights_ready, 1)
                        nc.tensor.matmul(z_ps[:, 0:128], wqk[:, 0, :], wqk[:, 1, :], start=True,
                                         stop=True).then_inc(a_written, 1)
                        pe.wait_ge(x_loaded[par], 32 * (img // 2 + 1))
                    else:
                        pe.wait_ge(x_loaded[par], 32 * (img // 2 + 1))
                    last = nc.tensor.matmul(bank[:, :], keep["w1c"], xin[:, par, ds(qb * BT + 1, BT), :],
                                            start=True, stop=True)
                elif name.startswith("tap"):
                    t = int(name[3:])
                    if full == "tap0@0":
                        pe.wait_ge(conv2_ready, 1)
                    if t == 0:
                        pe.wait_ge(conv1_low_ready, prepared)
                    last = nc.tensor.matmul(bank[:, :], conv2_w[:, t * 128:(t + 1) * 128], conv1_split[:, :],
                                            start=True, stop=True)
                elif name.startswith("pz"):
                    if name == "pz0":
                        pe.wait_ge(z_copied, body.posts(qb))
                    for j in range(2):
                        jj = 2 * int(name[2:]) + j
                        last = nc.tensor.matmul(bank[:, j * 130:(j + 1) * 130], z_sb[:, jj * 128:(jj + 1) * 128],
                                                wv_w[:, :], start=True, stop=True)
                elif name.startswith(("yt", "xt")):
                    src = y_block if name[0] == "y" else xn_block
                    if full == "xt@0":
                        pe.wait_ge(kept_loaded, 16)
                    if name == "yt":
                        pe.wait_ge(y_ready, body.posts(qb))
                    else:
                        pe.wait_ge(xn_ready, prepared)
                    for j in range(BT // 2):
                        last = nc.tensor.transpose(bank[:, j * 128:(j + 1) * 128],
                                                   src[:, 2 * j:2 * j + 2, :].rearrange("p a d -> p (a d)"), ident)
                elif name.startswith("g"):
                    c = int(name[1:])
                    if full == "g0@0":
                        pe.wait_ge(a_ready, 1)
                    xt = other(full, "xt")
                    pe.wait_ge(drained[body.bank[xt]], body.filled(xt, turn))
                    cols = keys_t[:, par, ds(qb * QB + c * 512, 512)]
                    nc.tensor.matmul(bank[:, :], a_high[:, :], cols, start=True, stop=False)
                    last = nc.tensor.matmul(bank[:, :], a_low[:, :], cols, start=False, stop=True)
                elif name.startswith("nm"):
                    c = int(name[2:])
                    pe.wait_ge(high_ready, body.highs(other(full, f"g{c}"), turn))
                    last = nc.tensor.matmul(bank[:, :], ones[:, :], g_square[:, c, :], start=True, stop=True)
                elif name == "lg":
                    pe.wait_ge(drained[body.bank["yt"]], body.filled("yt", qb))
                    for t in range(BT):
                        last = nc.tensor.matmul(bank[:, t * 64:(t + 1) * 64], y_t[:, t * 128:(t + 1) * 128],
                                                router_w[:, :, :].rearrange("p e s -> p (e s)"),
                                                start=True, stop=True)
                elif name.startswith("ot"):
                    pe.wait_ge(onehot_ready, body.posts(qb))
                    for j in range(BT // 4):
                        last = nc.tensor.transpose(bank[:, j * 128:(j + 1) * 128],
                                                   onehot[:, 4 * j:4 * j + 4, :].rearrange("p t e -> p (t e)"), ident)
                elif name.startswith("hid"):
                    f, c = divmod(int(name[3:]), 2)
                    pe.wait_ge(drained[body.bank["ot"]], body.filled("ot", qb))
                    rows = slice(f * 128, (f + 1) * 128)
                    cols = slice(c * 512, (c + 1) * 512)
                    nc.tensor.matmul(bank[:, :], w1_high[:, rows], y_t[:, cols], start=True, stop=False)
                    nc.tensor.matmul(bank[:, :], w1_low[:, rows], y_t[:, cols], start=False, stop=False)
                    last = nc.tensor.matmul(bank[:, :], mask_w[:, rows], onehot_t[:, cols], start=False, stop=True)
                elif name == "o2":
                    for f in range(FT):
                        for c in range(2):
                            pe.wait_ge(drained[body.bank[f"hid{2 * f + c}"]], body.filled(f"hid{2 * f + c}", qb))
                            nc.tensor.matmul(bank[64 * c:64 * c + 64, :], w2[:, f, :],
                                             hidden[:, f, c * 512:(c + 1) * 512], start=(f == 0), stop=False)
                    for c in range(2):
                        last = nc.tensor.matmul(bank[64 * c:64 * c + 64, :], keep["b2"],
                                                onehot_t[:, c * 512:(c + 1) * 512].bitcast(F32),
                                                start=False, stop=True)
                else:
                    pe.wait_ge(drained[body.bank["o2"]], body.filled("o2", qb))
                    for j in range(4):
                        last = nc.tensor.transpose(bank[:, j * 128:(j + 1) * 128],
                                                   o2_sb[:, j * 128:(j + 1) * 128], ident)
                last.then_inc(filled[k], 1)

            def score(way, b, kt, qb, block):
                before = block * TILES + (kt - 1)
                if later(before):
                    pe.wait_ge(way.probs_ready, before)
                lhs = keys_t[:, b % 2, kt * 128:(kt + 1) * 128]
                for c in range(2):
                    cols = query_cols(block, c)
                    dst = scores[:, kt % 2, c * 512:(c + 1) * 512]
                    nc.tensor.matmul(dst, lhs, g_high[:, cols], start=True, stop=False)
                    last = nc.tensor.matmul(dst, lhs, g_low[:, cols], start=False, stop=True)
                last.then_inc(way.scores_ready, 1)

            def into_z(keys_of_tile, kt):
                for c in range(2):
                    last = nc.tensor.matmul(z_ps[64 * c:64 * c + 64, :], keys_of_tile,
                                            probs[:, kt % RING, c * 512:(c + 1) * 512],
                                            start=(kt == 0), stop=(kt == TILES - 1))
                return last

            def weigh(way, keys_of_tile, kt, block):
                if kt == 0 and later(block):
                    pe.wait_ge(z_copied, block)
                pe.wait_ge(way.probs_ready, block * TILES + (kt + 1))
                into_z(keys_of_tile, kt).then_inc(way.pv_done, 1)

            def run(body, qb):
                par = body.b % 2
                for name in body.slots.get(-1, []):
                    fill(body, name, qb)
                if body is opening:
                    for name in ("g0@0", "g1@0"):
                        pe.wait_ge(drained[body.bank[name]], body.filled(name, qb))
                for g in range(TILES // 2):
                    if body.attend:
                        if body is opening and g * 2 % BT == 0:
                            name = f"xt@{g * 2 // BT}"
                            pe.wait_ge(drained[body.bank[name]], body.filled(name, qb))
                        score(usual, body.b, 2 * g, qb, body.block(qb))
                        score(usual, body.b, 2 * g + 1, qb, body.block(qb))
                    if g == 0 and body.post:
                        pe.wait_ge(last_keys_ready, (body.block(qb) + (NQ - 1)) // NQ)
                        for u in range(2):
                            weigh(usual, last_keys[:, u, :], TILES - 2 + u, body.block(qb) - 1)
                    for name in body.slots.get(g, []):
                        fill(body, name, qb)
                    if body.attend and g:
                        if body is opening and (2 * g - 2) % BT == 0:
                            pe.wait_ge(keys_ready, (2 * g - 2) // BT + 1)
                        for kt in (2 * g - 2, 2 * g - 1):
                            weigh(usual, keys[:, par, kt, :], kt, body.block(qb))
                for name in body.slots.get(TILES // 2, []):
                    fill(body, name, qb)

            def attend_again():
                for kt in (TILES - 2, TILES - 1):
                    into_z(keys[:, 0, kt, :], kt)
                for kt in range(TILES):
                    score(again, 0, kt, 0, 0)
                    if 0 < kt < TILES - 1:
                        weigh(again, keys[:, 0, kt - 1, :], kt - 1, 0)
                pe.wait_ge(again.probs_ready, TILES)

            def find_max(b, after):
                def tile(r):
                    for u in range(2):
                        pe.wait_ge(g_tile_ready, (r + 16 * b) * 2 + (u + 1))
                        for part in range(4):
                            before = (r + 16 * b) * 8 + (4 * u + part - 1)
                            if later(before):
                                pe.wait_ge(max_scores_read, before)
                            for c in range(2):
                                k0 = part * QB + c * 512
                                last = nc.tensor.matmul(scores[:, part % 2, c * 512:(c + 1) * 512],
                                                        g_tile[:, u, :], keys_t[:, b % 2, k0:k0 + 512],
                                                        start=True, stop=True)
                            last.then_inc(max_scores_ready, 1)

                def shift(r):
                    for u in range(2):
                        pe.wait_ge(diag_ready, (r + 4 * b) * 2 + (u + 1))
                        before = (r + 4 * b) * 2 + (u - 1)
                        if later(before):
                            pe.wait_ge(shifted_split, before)
                        cols = keys_t[:, b % 2, ds(r * QB + u * 512, 512)]
                        nc.tensor.matmul(banks[u][:, :], a_high[:, :], cols, start=True, stop=False)
                        nc.tensor.matmul(banks[u][:, :], a_low[:, :], cols, start=False, stop=False)
                        nc.tensor.matmul(banks[u][:, :], keep["e0"],
                                         diag[:, u, :, :].rearrange("p j n -> p (j n)"),
                                         start=False, stop=True).then_inc(shifted_ready, 1)

                for k in range(NBANK):
                    pe.wait_ge(drained[k], after.start[k])
                pe.wait_ge(usual.probs_ready, max(TILES * NQ * b, TILES))
                tile(0)
                with pe.Fori(1, TILES // 2) as r:
                    tile(r)
                shift(0)
                with pe.Fori(1, NQ) as r:
                    shift(r)
                pe.wait_ge(max_scores_read, 128 * (b + 1))
                pe.wait_ge(shifted_split, 8 * (b + 1))

            def shift_if_needed(b, after):
                pe.wait_ge(flag_ready, NQ * (b + 1))
                with pe.If(pe.value_load(flag[0:1, 0:1], min_val=0, max_val=1)):
                    find_max(b, after)
                    if b == 0:
                        attend_again()
                with pe.Else():
                    pe.sem_inc(max_scores_ready, 4 * TILES)
                    pe.sem_inc(shifted_ready, S // 512)

            pe.wait_ge(kept_first_loaded, 16)
            run(opening, 0)
            shift_if_needed(0, rest[0])
            for body, before in zip(rest, plan):
                if 0 < body.b < B:
                    for name in ("xt", "g0", "g1"):
                        pe.wait_ge(drained[before.bank[name]], before.filled(name, NQ - 1))
                    pe.wait_ge(keys_ready, NQ * (body.b + 1))
                    shift_if_needed(body.b, body)
                each_block(pe, body, lambda qb: run(body, qb))
            run(epilogue, 0)

        @block.scalar
        def _(act):
            def drain(body, full, turn):
                k = body.bank[full]
                bank = banks[k]
                name, qb = base(full), turn
                if name.startswith(PRE):
                    img, qb, prepared = body.prepares(full, turn)
                    par = img % 2
                if name == "c1":
                    act.wait_ge(filled[k], body.filled(full, turn))
                    nc.scalar.activation(conv1_split[:, :], bank[:, :], ACT.Relu, bias=bn[:, 1:2], scale=bn[:, 0:1])
                    nc.scalar.activation(conv1_full[64:128, :], bank[64:128, :], ACT.Relu, bias=bn[64:128, 1:2],
                                         scale=bn[64:128, 0:1]).then_inc(drained[k], 1)
                    if full == "c1@1":
                        act.wait_ge(a_written, 1)
                        nc.scalar.copy(a_high[:, :], z_ps[:, 0:128]).then_inc(a_high_ready, 1)
                elif name.startswith(("yt", "xt")):
                    act.wait_ge(filled[k], body.filled(full, turn))
                    dst = by_parity(y_t[0:64, :] if name[0] == "y" else keys_t[0:64, par, ds(qb * QB, QB)])
                    for odd in range(2):
                        nc.scalar.copy(dst[:, :, odd, :], bank[64 * odd:64 * odd + 64, :].rearrange(
                            "p (t q) -> p t q", q=128)).then_inc(high_ready, 1)
                elif name.startswith("g"):
                    act.wait_ge(filled[k], body.filled(full, turn))
                    c = int(name[1:])
                    nc.scalar.activation(g_square[:, c, :], bank[:, :], ACT.Square)
                    nc.scalar.copy(g_high[:, query_cols(prepared - 1, c)], bank[:, :]).then_inc(high_ready, 1)
                elif name.startswith("ot"):
                    act.wait_ge(filled[k], body.filled(full, turn))
                    dst = onehot_t[0:E, :].rearrange("p (j t q) -> p j t q", t=4, q=128)
                    src = bank[:, 0:BT // 4 * 128].rearrange("p (j q) -> p j q", q=128)
                    for t in range(4):
                        last = nc.scalar.copy(dst[:, :, t, :], src[t * E:(t + 1) * E])
                    last.then_inc(drained[k], 1)
                elif name.startswith("hid"):
                    act.wait_ge(filled[k], body.filled(full, turn))
                    f, c = divmod(int(name[3:]), 2)
                    nc.scalar.activation(hidden[:, f, c * 512:(c + 1) * 512], bank[:, :],
                                         ACT.Relu).then_inc(drained[k], 1)

            def exponentiate(way, kt, block, scale=SCALE):
                n = block * TILES
                act.wait_ge(way.scores_ready, n + (kt + 1))
                if later(n + (kt + 1 - RING)):
                    act.wait_ge(way.pv_done, n + (kt + 1 - RING))
                nc.scalar.activation(probs[:, kt % RING, :], scores[:, kt % 2, :], ACT.Exp,
                                     scale=scale).then_inc(way.probs_ready, 1)

            def run(body, qb):
                for g in range(-1, TILES // 2 + 1):
                    if body.attend and 0 <= g < TILES // 2:
                        for kt in (2 * g, 2 * g + 1):
                            if body is opening and kt == 0:
                                act.wait_ge(first_scale_ready, 1)
                            exponentiate(usual, kt, body.block(qb), first_scale[:, 0:1] if body is opening else SCALE)
                    for name in body.slots.get(g, []):
                        drain(body, name, qb)

            def find_max(b):
                def tile(r, first_tile):
                    for u in range(2):
                        if not first_tile:
                            act.wait_ge(max_scores_ready, (r + 16 * b) * 8 + (4 * u - 4))
                        block, t = (r * 2 + u) // BT + NQ * b, (r * 2 + u) % BT
                        nc.scalar.copy(g_tile[:, u, :], g_high[:, ds(block % (NQ + 1) * QB + t * 128, 128)]
                                       ).then_inc(g_tile_ready, 1)

                def shift(r):
                    for u in range(2):
                        act.wait_ge(shifted_ready, (r + 4 * b) * 2 + (u + 1))
                        nc.scalar.copy(g_high[:, query_cols(r + NQ * b, u)], banks[u][:, :]
                                       ).then_inc(shifted_high_ready, 1)

                act.drain()
                tile(0, True)
                with act.Fori(1, TILES // 2) as r:
                    tile(r, False)
                with act.Fori(0, NQ) as r:
                    shift(r)
                act.drain()

            def shift_if_needed(b):
                act.wait_ge(flag_ready, NQ * (b + 1))
                with act.If(act.value_load(flag[0:1, 0:1], min_val=0, max_val=1)):
                    find_max(b)
                    if b == 0:
                        for kt in range(TILES):
                            exponentiate(again, kt, 0)
                with act.Else():
                    act.sem_inc(g_tile_ready, TILES)
                    act.sem_inc(shifted_high_ready, S // 512)

            act.wait_ge(once_loaded, 16)
            nc.scalar.copy(conv2_w[:, :], load["w2c"]).then_inc(weights_high_ready, 1)
            act.wait_ge(bn_ready, 1)
            run(opening, 0)
            shift_if_needed(0)
            for body in rest:
                if 0 < body.b < B:
                    shift_if_needed(body.b)
                each_block(act, body, lambda qb: run(body, qb))
            run(epilogue, 0)

        @block.vector
        def _(dve):
            V = nc.vector

            def settle():
                dve.drain()

            def wide(v, n):
                return v.unsqueeze(v.ndim).broadcast_to([*v.shape, n])

            def rsqrt(dst, v, half):
                V.tensor_scalar(half.bitcast(I32), v.bitcast(I32), 1, None, ALU.logical_shift_right)
                settle()
                V.tensor_scalar(dst.bitcast(I32), half.bitcast(I32), -1.0, RSQRT_SEED, ALU.mult, ALU.add)
                settle()
                for _ in range(3):
                    V.scalar_tensor_tensor(half, dst, -0.5, dst, ALU.mult, ALU.mult)
                    settle()
                    V.tensor_tensor(half, half, v, ALU.mult)
                    settle()
                    V.scalar_tensor_tensor(dst, half, 1.5, dst, ALU.add, ALU.mult)
                    settle()

            total, var, scratch, rstd = (stat[:, k, :] for k in range(4))

            def normalise(src):
                V.reduce_sum(total, src, AX_X)
                settle()
                V.scalar_tensor_tensor(centred[:, :, :], wide(total, D), -1.0 / D, src, ALU.mult, ALU.add)
                settle()
                V.tensor_tensor(squares[:, :, :], centred[:, :, :], centred[:, :, :], ALU.mult)
                settle()
                V.reduce_sum(total, squares[:, :, :], AX_X)
                settle()
                V.tensor_scalar(var, total, 1.0 / D, EPS, ALU.mult, ALU.add)
                settle()
                rsqrt(rstd, var, scratch)

            def write_normalised(dst):
                return V.tensor_tensor(dst[:, :, 1:D], centred[:, :, 1:D], wide(rstd, D - 1), ALU.mult)

            def residual(body, qb):
                slot = qb + (NQ * (body.b % 2) + 2 * NQ - 1)
                return hres[:, ds(slot % (2 * NQ) * BT, BT), :]

            def layernorm(block, prepared):
                settle()
                normalise(block)
                if later(prepared - 1):
                    dve.wait_ge(keys_ready, prepared - 1)
                write_normalised(xn_block).then_inc(xn_ready, 1)

            def drain(body, full, turn):
                k = body.bank[full]
                bank = banks[k]
                name, qb = base(full), turn
                if name.startswith(PRE):
                    img, qb, prepared = body.prepares(full, turn)
                    par = img % 2
                if name == "c1":
                    dve.wait_ge(drained[k], body.filled(full, turn))
                    V.tensor_tensor(conv1_split[64:128, :], conv1_full[64:128, :],
                                    conv1_split[64:128, :].bitcast(F32), ALU.subtract).then_inc(conv1_low_ready, 1)
                    if full == "c1@0":
                        dve.wait_ge(qk_loaded, 16)
                        V.tensor_tensor(wqk[:, 0, :], load["wqm"][0:64], load["wqb"][0:64], ALU.subtract)
                        V.tensor_tensor(wqk[:, 1, :], load["wkm"][0:64], load["wkb"][0:64],
                                        ALU.subtract).then_inc(qk_weights_ready, 1)
                    elif full == "c1@1":
                        dve.wait_ge(a_high_ready, 1)
                        V.tensor_tensor(a_low[:, :], z_ps[:, 0:128], a_high[:, :].bitcast(F32),
                                        ALU.subtract).then_inc(a_ready, 1)
                    if body is opening and prepared > 1:
                        layernorm(hres[:, (prepared - 2) * BT:(prepared - 1) * BT, :], prepared - 1)
                elif name.startswith("tap"):
                    t = int(name[3:])
                    mine = hres[:, ds(qb * BT + par * TILES, BT), :]
                    dh, dw = divmod([4, 0, 1, 2, 3, 5, 6, 7, 8][t], 3)
                    lo, hi = max(0, 1 - dw), min(W, W + 1 - dw)
                    flt = bank[:, :].rearrange("p (r w) -> p r w", w=W)[:, :, lo:hi]
                    pix = xin[:, par, ds(qb * BT + dh, BT), lo + dw - 1:hi + dw - 1]
                    dst = mine if t == 0 else tap_product[:, t % 2, :, lo:hi]
                    if full == "tap0@0":
                        dve.wait_ge(x_first_loaded, 32)
                    elif t == 0:
                        dve.wait_ge(x_loaded[par], 32 * (img // 2 + 1))
                    dve.wait_ge(filled[k], body.filled(full, turn))
                    V.scalar_tensor_tensor(dst, flt, keep["b2c"][:, t:t + 1], pix, ALU.add,
                                           ALU.mult).then_inc(drained[k], 1)
                    settle()
                    if t:
                        V.tensor_tensor(mine[:, :, lo:hi], mine[:, :, lo:hi], dst, ALU.add)
                    if t == TAPS - 1 and (body is not opening or prepared == NQ):
                        layernorm(mine, prepared)
                elif name.startswith(("yt", "xt")):
                    high, low = (by_parity(y_t[r, :] if name[0] == "y" else keys_t[r, par, ds(qb * QB, QB)])
                                 for r in (slice(0, 64), slice(64, 128)))
                    for odd in range(2):
                        dve.wait_ge(high_ready, body.highs(full, turn, odd))
                        last = V.tensor_tensor(low[:, :, odd, :], bank[64 * odd:64 * odd + 64, :].rearrange(
                            "p (t q) -> p t q", q=128), high[:, :, odd, :].bitcast(F32), ALU.subtract)
                    last.then_inc(drained[k], 1)
                elif name.startswith("g"):
                    cols = query_cols(prepared - 1, int(name[1:]))
                    dve.wait_ge(high_ready, body.highs(full, turn))
                    V.tensor_tensor(g_low[:, cols], bank[:, :], g_high[:, cols].bitcast(F32),
                                    ALU.subtract).then_inc(drained[k], 1)
                elif name.startswith("nm"):
                    dve.wait_ge(filled[k], body.filled(full, turn))
                    V.reduce_max(norm_max[:, par, ds(qb * 2 + int(name[2:]), 1)], bank[:, :],
                                 AX_X).then_inc(drained[k], 1)
                    if name == "nm1":
                        raise_flag(par)
                    if full == "nm1@0":
                        worst = stat[:, 7, 0:1]
                        settle()
                        V.reduce_max(worst, norm_max[:, 0, 0:2], AX_X)
                        settle()
                        V.tensor_scalar(first_scale[:, :], worst, NORM_LIMIT, SCALE, ALU.is_le,
                                        ALU.mult).then_inc(first_scale_ready, 1)
                elif name.startswith("pz"):
                    n = int(name[2:])
                    dve.wait_ge(filled[k], body.filled(full, turn))
                    both = bank[:, 0:260].rearrange("p (j a w) -> p j a w", j=2, a=2)
                    rs = stat[:, 4, :].rearrange("p (a j) -> p j a", a=2)[:, 2 * n:2 * n + 2, :]
                    V.reciprocal(rs, both[:, :, :, D])
                    settle()
                    rows = h2[:, :, :].rearrange("p (a j) w -> p j a w", a=2)[:, 2 * n:2 * n + 2]
                    V.tensor_tensor(rows, both[:, :, :, 0:D], wide(rs, D), ALU.mult).then_inc(drained[k], 1)
                    if n:
                        settle()
                        V.tensor_tensor(h2[:, :, :], h2[:, :, :], residual(body, qb), ALU.add)
                        settle()
                        normalise(h2[:, :, :])
                        write_normalised(y_block).then_inc(y_ready, 1)
                elif name == "lg":
                    dve.wait_ge(filled[k], body.filled(full, turn))
                    V.reduce_sum(logits[:, :, :], bank[:, :].rearrange("p (t e s) -> p t e s", t=BT, s=2),
                                 AX_X).then_inc(drained[k], 1)
                    settle()
                    best = stat[:, 5, :]
                    V.reduce_max(best, logits[:, :, :], AX_X)
                    settle()
                    V.tensor_tensor(pick[:, :, :], logits[:, :, :], wide(best, E), ALU.is_ge)
                    settle()
                    V.tensor_tensor(pick[:, :, :], pick[:, :, :],
                                    keep["desc"].unsqueeze(1).broadcast_to([128, BT, E]), ALU.mult)
                    settle()
                    V.reduce_max(best, pick[:, :, :], AX_X)
                    settle()
                    V.tensor_tensor(onehot[:, :, :], pick[:, :, :], wide(best, E),
                                    ALU.is_equal).then_inc(onehot_ready, 1)
                elif name == "o2":
                    dve.wait_ge(filled[k], body.filled(full, turn))
                    V.tensor_copy(o2_sb[:, :], bank[:, :]).then_inc(drained[k], 1)
                elif name == "fin":
                    dve.wait_ge(filled[k], body.filled(full, turn))
                    dve.wait_ge(out_sb_free, body.posts(qb))
                    both = bank[:, :].rearrange("p (j a w) -> p j a w", j=4, a=2)
                    for a in range(2):
                        tiles = slice(4 * a, 4 * a + 4)
                        last = V.scalar_tensor_tensor(out_sb[:, tiles, :], both[:, :, a, :], 0.0, h2[:, tiles, :],
                                                      ALU.max, ALU.add)
                    last.then_inc(drained[k], 1)
                    settle()
                    V.engine_nop().then_inc(out_ready, 1)

            def run(body, qb):
                if body.post:
                    dve.wait_ge(usual.pv_done, body.posts(qb) * TILES)
                    V.tensor_copy(z_sb[:, :], z_ps[:, :]).then_inc(z_copied, 1)
                for g in range(-1, TILES // 2 + 1):
                    for name in body.slots.get(g, []):
                        drain(body, name, qb)

            def find_max(b):
                def tile(r):
                    for u in range(2):
                        for part in range(4):
                            dve.wait_ge(max_scores_ready, (r + 16 * b) * 8 + (4 * u + part + 1))
                            V.reduce_max(max4[:, u, part:part + 1], scores[:, part % 2, :],
                                         AX_X).then_inc(max_scores_read, 1)
                        settle()
                        V.tensor_reduce(neg_max[:, ds(r * 2 + u, 1)], max4[:, u, :], AX_X, ALU.max, negate=True)

                def shift(r):
                    for u in range(2):
                        if later((r + 4 * b) * 2 + (u - 1)):
                            dve.wait_ge(shifted_ready, (r + 4 * b) * 2 + (u - 1))
                        V.tensor_tensor(diag[:, u, :, :], ident.unsqueeze(1).broadcast_to([128, 4, 128]),
                                        wide(neg_max[:, ds((r * 2 + u) * 4, 4)], 128), ALU.mult
                                        ).then_inc(diag_ready, 1)
                    for u in range(2):
                        cols = query_cols(r + NQ * b, u)
                        dve.wait_ge(shifted_high_ready, (r + 4 * b) * 2 + (u + 1))
                        V.tensor_tensor(g_low[:, cols], banks[u][:, :], g_high[:, cols].bitcast(F32),
                                        ALU.subtract).then_inc(shifted_split, 1)

                with dve.Fori(0, TILES // 2) as r:
                    tile(r)
                settle()
                shift(0)
                with dve.Fori(1, NQ) as r:
                    shift(r)

            def raise_flag(par):
                worst = stat[:, 6, 0:1]
                settle()
                V.reduce_max(worst, norm_max[:, par, :], AX_X)
                settle()
                V.tensor_scalar(flag[:, :], worst, NORM_LIMIT, None, ALU.is_gt).then_inc(flag_ready, 1)

            def shift_if_needed(b):
                dve.wait_ge(flag_ready, NQ * (b + 1))
                with dve.If(dve.value_load(flag[0:1, 0:1], min_val=0, max_val=1)):
                    find_max(b)
                with dve.Else():
                    dve.sem_inc(max_scores_read, 4 * TILES)
                    dve.sem_inc(diag_ready, S // 512)
                    dve.sem_inc(shifted_split, S // 512)

            for par in range(2):
                V.memset(xin[0:64, par, 0:1, :], 0.0)
                V.memset(xin[64:128, par, TILES + 1:TILES + 2, :], 0.0)
            dve.wait_ge(kept_first_loaded, 16)
            V.tensor_scalar(bn[:, 2:3], keep["bn"][:, 4:5], EPS, None, ALU.add)
            V.tensor_tensor(bn[:, 5:6], keep["bn"][:, 0:1], keep["bn"][:, 1:2], ALU.subtract)
            settle()
            rsqrt(bn[:, 3:4], bn[:, 2:3], bn[:, 4:5])
            V.tensor_tensor(bn[:, 0:1], bn[:, 3:4], keep["bn"][:, 2:3], ALU.mult)
            settle()
            V.scalar_tensor_tensor(bn[:, 1:2], bn[:, 5:6], bn[:, 0:1], keep["bn"][:, 3:4], ALU.mult,
                                   ALU.add).then_inc(bn_ready, 1)
            dve.wait_ge(weights_high_ready, 1)
            for p in (32, 96):
                rows = slice(p, p + 32)
                last = V.tensor_tensor(conv2_w[rows, :], load["w2c"][rows], conv2_w[rows, :].bitcast(F32),
                                       ALU.subtract)
            last.then_inc(conv2_ready, 1)
            dve.wait_ge(constants_ready, 1)

            run(opening, 0)
            shift_if_needed(0)
            dve.wait_ge(pool_weights_ready, 1)
            for body in rest:
                if 0 < body.b < B:
                    shift_if_needed(body.b)
                each_block(dve, body, lambda qb: run(body, qb))
            run(epilogue, 0)


def _pack(parts, at, n):
    buf = np.zeros((128, n), np.float32)
    for name, a in parts.items():
        lo, hi = at[name]
        buf[:a.shape[0], lo:hi] = a.reshape(a.shape[0], -1)
    return buf


def _less_row0(w, bias):
    main, base = np.array(w), np.zeros_like(w)
    main[0] = bias
    base[1:] = w[0:1]
    return main, base


def kernel(**inputs):
    import concourse.bacc as _bacc
    from concourse.bass_utils import run_bass_kernel_spmd as _run

    a = {k: np.asarray(v) for k, v in inputs.items()}

    qm, qs = _less_row0(a["L0_attn_Wq"], a["L0_attn_bq"])
    km, ks = _less_row0(a["L0_attn_Wk"], a["L0_attn_bk"])
    vm, vs = _less_row0(a["L0_attn_Wv"], a["L0_attn_bv"])
    rm, rs = _less_row0(np.ascontiguousarray(a["L0_ffn_router_w"].T), a["L0_ffn_router_b"])
    w1 = np.ascontiguousarray(a["L0_ffn_W1"].transpose(1, 0, 2)).reshape(D, E * H)
    w1m, w1s = _less_row0(w1, a["L0_ffn_b1"].reshape(-1))

    def twice(m, axis):
        return np.concatenate([m, m], axis)

    def value_diag(m, one):
        v = np.zeros((128, 130), np.float32)
        for k in range(2):
            v[64 * k:64 * k + 64, 65 * k:65 * k + 64] = m
            v[64 * k, 65 * k + 64] = one
        return v

    order = [4, 0, 1, 2, 3, 5, 6, 7, 8]
    w2c = np.zeros((4, HH, O, TAPS, HH, C), np.float32)
    w1c = np.zeros((HH, C, 4, HH, O), np.float32)
    for h in range(HH):
        w2c[:, h, :, :, h, :] = a["L0_tok_conv2_w"][order].T[None, :, :, None]
        w1c[h, :, :, h, :] = a["L0_tok_conv1_w"].T[:, None, :]
    mask = np.full((E, E, H), -BIG, np.float32)
    mask[np.arange(E), np.arange(E)] = 0.0
    bn = np.stack([a["L0_tok_" + n] for n in ("conv1_b", "bn_mean", "bn_gamma", "bn_beta", "bn_var")], 1)
    e0 = np.zeros((128, 128), np.float32)
    e0[:, 0] = e0[:, 64] = 1.0

    once = _pack(dict(w2c=w2c.reshape(128, -1), w1m=twice(w1m, 0), w1b=twice(w1s, 0),
                      mask=mask.reshape(E, E * H), rm=twice(rm, 0), rb=twice(rs, 0),
                      wvm=value_diag(vm, 1.0), wvb=value_diag(vs, 0.0),
                      wqm=twice(qm.T, 1), wqb=twice(qs.T, 1), wkm=twice(km.T, 1), wkb=twice(ks.T, 1)),
                 ONCE_AT, ONCE_N)
    w2 = a["L0_ffn_W2"].reshape(FT, 128, D).transpose(1, 0, 2)
    kept = _pack(dict(ident=np.eye(128, dtype=np.float32), w1c=w1c.reshape(128, 128), w2=w2,
                      b2=a["L0_ffn_b2"], desc=np.tile(np.arange(E, 0, -1, dtype=np.float32), (128, 1)),
                      bn=np.tile(bn, (8, 1)), b2c=np.tile(a["L0_tok_conv2_b"][order], (128, 1)), e0=e0),
                 KEPT_AT, KEPT_N)

    nc = _bacc.Bacc("TRN2", target_bir_lowering=False, num_devices=1)
    arrays = {"x_dram": np.ascontiguousarray(a["x"]), "once_dram": once, "kept_dram": kept}
    args = [nc.dram_tensor(n, v.shape, F32, kind="ExternalInput").ap() for n, v in arrays.items()]
    out = nc.dram_tensor("out_dram", (B, S, D), F32, kind="ExternalOutput").ap()
    vit_block_kernel(nc, *args, out)
    r = _run(nc, [arrays], core_ids=[0])
    return r.results[0]["out_dram"]
```
